# Optimizing a Trainium2 kernel written in Bass

```python
import numpy as np
import jax
import jax.numpy as jnp

def _softmax(x, axis=-1):
    return jax.nn.softmax(x, axis=axis)

def _gelu(x):
    return jax.nn.gelu(x, approximate=True)

def _silu(x):
    return jax.nn.silu(x)

def _sigmoid(x):
    return jax.nn.sigmoid(x)

def _layernorm(x, axis=-1, eps=1e-05):
    m = jnp.mean(x, axis=axis, keepdims=True)
    v = jnp.var(x, axis=axis, keepdims=True)
    return (x - m) / jnp.sqrt(v + eps)

def _scatter_add(tgt, idx, src, axis=0):
    return tgt.at[idx].add(src)

def _segment_sum(src, seg, n):
    return jax.ops.segment_sum(src, seg, n)
kernel_name = 'mk_flamingo_gated_d1_seqx_r8_191c3a'

def setup_inputs(seed: int=0):
    np.random.seed(seed)
    _w = jnp.asarray

    def _rec_inputs():
        import jax
        import jax.numpy as jnp
        _rk = jax.random.key(seed)
        x = -0.0002928 + 1 * jax.random.normal(jax.random.fold_in(_rk, 1), (64, 128, 128), jnp.float32)
        _lenS = 128 - jax.random.randint(jax.random.fold_in(_rk, 7), (64,), 0, max(1, 128 // 4) + 1, jnp.int32)
        _lenS2 = 77 - jax.random.randint(jax.random.fold_in(_rk, 8), (64,), 0, max(1, 77 // 4) + 1, jnp.int32)
        _ctx_1024P = jax.random.normal(jax.random.fold_in(_rk, 11), (64, 16, 128), jnp.float32)
        _ctx_1024c = jax.random.dirichlet(jax.random.fold_in(_rk, 511), 0.3 * jnp.ones((16,), jnp.float32), (64, 77))
        _ctx_1024t = jnp.einsum('bsk,bkd->bsd', _ctx_1024c, _ctx_1024P)
        _ctx_1024t = _ctx_1024t * jax.lax.rsqrt(jnp.mean(jnp.square(_ctx_1024t)) + 1e-12) * 0.953939
        ctx_1024 = -1.39393e-06 + 0.999914 * (_ctx_1024t + 0.3 * jax.random.normal(jax.random.fold_in(_rk, 611), (64, 77, 128), jnp.float32))
        _g = jax.random.normal(jax.random.fold_in(_rk, 9001), (2, 1), jnp.float32)
        _g = jnp.sign(_g) * jnp.maximum(jnp.abs(_g), 1.0) + (_g == 0) * 1.0
        g_xattn = _g[0]
        g_ffn = _g[1]
        return (x, ctx_1024, g_xattn, g_ffn)
    x, ctx_1024, g_xattn, g_ffn = _rec_inputs()

    def _L0_xattn_setup():
        import jax, jax.numpy as jnp
        import numpy as np
        D_MODEL = 128
        NUM_HEADS = 16
        DEPTH = D_MODEL // NUM_HEADS
        key = jax.random.key(seed)
        ks = jax.random.split(key, 6)
        B, S = (2, 256)
        scale = 1.0 / np.sqrt(D_MODEL)
        return {'q': jax.random.normal(ks[0], (B, S, D_MODEL), jnp.float32), 'k': jax.random.normal(ks[1], (B, S, D_MODEL), jnp.float32), 'v': jax.random.normal(ks[2], (B, S, D_MODEL), jnp.float32), 'wq': jax.random.normal(ks[3], (D_MODEL, D_MODEL), jnp.float32) * scale, 'wk': jax.random.normal(ks[4], (D_MODEL, D_MODEL), jnp.float32) * scale, 'wv': jax.random.normal(ks[5], (D_MODEL, D_MODEL), jnp.float32) * scale}
    _L0_xattn_all = _L0_xattn_setup()
    _L0_xattn_in = {k: v for k, v in _L0_xattn_all.items() if k in ('wq', 'wk', 'wv')}
    del _L0_xattn_all

    def _L0_ffn_setup():
        import jax, jax.numpy as jnp
        import numpy as np
        B, T, D, E, K = (2, 256, 128, 8, 2)
        H = 2 * D
        key = jax.random.key(seed)
        ks = jax.random.split(key, 5)
        s = 0.02
        return {'x': jax.random.normal(ks[0], (B, T, D), jnp.float32), 'Wr': jax.random.normal(ks[1], (D, E), jnp.float32) * s, 'br': jnp.zeros((E,), jnp.float32), 'W1': jax.random.normal(ks[2], (E, D, H), jnp.float32) * s, 'b1': jnp.zeros((E, H), jnp.float32), 'W2': jax.random.normal(ks[3], (E, H, D), jnp.float32) * s, 'b2': jnp.zeros((E, D), jnp.float32)}
    _L0_ffn_all = _L0_ffn_setup()
    _L0_ffn_in = {k: v for k, v in _L0_ffn_all.items() if k in ('Wr', 'br', 'W1', 'b1', 'W2', 'b2')}
    del _L0_ffn_all
    return {'x': x, 'ctx_1024': ctx_1024, 'g_xattn': g_xattn, 'g_ffn': g_ffn, 'L0_xattn_wq': _L0_xattn_in['wq'], 'L0_xattn_wk': _L0_xattn_in['wk'], 'L0_xattn_wv': _L0_xattn_in['wv'], 'L0_ffn_Wr': _L0_ffn_in['Wr'], 'L0_ffn_br': _L0_ffn_in['br'], 'L0_ffn_W1': _L0_ffn_in['W1'], 'L0_ffn_b1': _L0_ffn_in['b1'], 'L0_ffn_W2': _L0_ffn_in['W2'], 'L0_ffn_b2': _L0_ffn_in['b2']}

def reference(x, ctx_1024, g_xattn, g_ffn, L0_xattn_wq, L0_xattn_wk, L0_xattn_wv, L0_ffn_Wr, L0_ffn_br, L0_ffn_W1, L0_ffn_b1, L0_ffn_W2, L0_ffn_b2):
    import jax
    import jax.numpy as jnp

    def _L0_xattn_ref(q, k, v, wq, wk, wv):
        import jax, jax.numpy as jnp
        import numpy as np
        D_MODEL = 128
        NUM_HEADS = 16
        DEPTH = D_MODEL // NUM_HEADS
        B, S, _ = q.shape

        def split(x):
            return x.reshape(B, -1, NUM_HEADS, DEPTH).transpose(0, 2, 1, 3)
        Q = split(q @ wq.T)
        K = split(k @ wk.T)
        V = split(v @ wv.T)
        scores = jnp.einsum('bhqd,bhkd->bhqk', Q, K) / np.sqrt(DEPTH).astype(np.float32)
        attn = jax.nn.softmax(scores, axis=-1)
        out = jnp.einsum('bhqk,bhkd->bhqd', attn, V)
        return out.transpose(0, 2, 1, 3).reshape(B, S, D_MODEL)

    def _L0_ffn_ref(x, Wr, br, W1, b1, W2, b2):
        import jax, jax.numpy as jnp
        import numpy as np
        B, T, D, E, K = (2, 256, 128, 8, 2)
        H = 2 * D
        logits = jnp.einsum('btd,de->bte', x, Wr) + br
        topv, topi = jax.lax.top_k(logits, K)
        sel_mask = jax.nn.one_hot(topi, E, dtype=logits.dtype).sum(-2) > 0
        neg_inf = jnp.finfo(logits.dtype).min
        gates = jax.nn.softmax(jnp.where(sel_mask, logits, neg_inf), axis=-1)
        h = jax.nn.relu(jnp.einsum('btd,edh->bteh', x, W1) + b1)
        out = jnp.einsum('bte,bteh,ehd->btd', gates, h, W2)
        out = out + jnp.einsum('bte,ed->btd', gates, b2)
        return out
    x = x + jnp.tanh(g_xattn[0]) * _L0_xattn_ref(_layernorm(x, axis=-1), ctx_1024, ctx_1024, L0_xattn_wq, L0_xattn_wk, L0_xattn_wv)
    x = x + jnp.tanh(g_ffn[0]) * _L0_ffn_ref(_layernorm(x, axis=-1), L0_ffn_Wr, L0_ffn_br, L0_ffn_W1, L0_ffn_b1, L0_ffn_W2, L0_ffn_b2)
    return x

_drawn_inputs = setup_inputs


def setup_inputs(seed=0):
    import zlib

    import numpy as np

    out = dict(_drawn_inputs(seed))
    spreads = {'L0_ffn_br': (0.0, 0.1), 'L0_ffn_b1': (0.0, 0.626), 'L0_ffn_b2': (0.0, 0.1)}
    factors = {}
    for name, (base, spread) in spreads.items():
        noise = np.random.default_rng([zlib.crc32(name.encode()), seed]).standard_normal(out[name].shape)
        drawn = base * np.exp(spread * noise) if base else spread * noise
        out[name] = jnp.asarray(drawn.astype(out[name].dtype))
    for name, factor in factors.items():
        out[name] = (out[name] * factor).astype(out[name].dtype)
    return out
```

```python
from contextlib import ExitStack

import concourse.bass as bass
from concourse import mybir

ALU = mybir.AluOpType
ACT = mybir.ActivationFunctionType
AXIS_X = mybir.AxisListType.X
F32 = mybir.dt.float32
BF16 = mybir.dt.bfloat16
U32 = mybir.dt.uint32

EPS = 1e-5
HEAD_ROWS = 32
ATT_LAG = 2
GROUP_LAG = 6
EXPERT_LAG = 7


def upper(ap):
    return ap.bitcast(BF16).rearrange("p (n t) -> p n t", t=2)[:, :, 1]


def due(count):
    return not isinstance(count, int) or count > 0


def flamingo_kernel(nc, x, ctx_t, g_xattn, g_ffn, wq_t, wkv_t, w_router, b_router, w1, b1, w2, b2, out):
    B, S, D = x.shape
    GROUPS, _, KEYS4 = ctx_t.shape
    NB = B // GROUPS
    KEYS = KEYS4 // NB
    KEYS_E = KEYS + KEYS % 2
    HEADS, DEPTH = 16, D // 16
    PER = 128 // HEAD_ROWS
    HG = HEADS // PER
    E = w_router.shape[1]
    HID = w1.shape[1] // E
    HC = HID // 128
    TOK = NB * S
    VW = 2 * DEPTH + 1
    SCALE = 1.0 / float(DEPTH) ** 0.5
    assert S == 128 and D == 128 and PER * HG == HEADS and E == 2 * NB
    SLOTS = B + EXPERT_LAG + 1
    BODY = 2 * NB
    FIRST = EXPERT_LAG + NB + 1
    LAST = B - NB
    assert (LAST - FIRST) % BODY == 0

    with ExitStack() as stack:
        def sb(name, shape, dt=F32):
            return stack.enter_context(nc.sbuf_tensor(name, shape, dt))

        def sem(name):
            return stack.enter_context(nc.semaphore(name))

        ident = sb("ident", [128, 128])
        ident_b = sb("ident_b", [128, 128], BF16)
        wq_sb = sb("wq_sb", [128, D])
        wkv_sb = sb("wkv_sb", [128, 2 * D])
        w1_sb = sb("w1_sb", [128, E * HID])
        w1_lo = sb("w1_lo", [128, E * HID], BF16)
        w2_sb = sb("w2_sb", [128, E * HC * D])
        w2_lo = sb("w2_lo", [128, E * HC * D], BF16)
        wr_sb = sb("wr_sb", [128, E])
        wr_rest = sb("wr_rest", [128, E])
        wr_rest2 = sb("wr_rest2", [128, E])
        wr3 = sb("wr3", [128, 3, E], BF16)
        br_sb = sb("br_sb", [128, E])
        b1_sb = sb("b1_sb", [128, E * HC])
        b2_rows = sb("b2_rows", [96, E * D])
        b2_rest = sb("b2_rest", [96, E * D])
        b2_rest2 = sb("b2_rest2", [96, E * D])
        b2_mid = sb("b2_mid", [96, E * D], BF16)
        b2_split = sb("b2_split", [96, E * D], BF16)
        ones_b = sb("ones_b", [96, 128], BF16)
        gates_in = sb("gates_in", [128, 2])
        tanh_g = sb("tanh_g", [128, 2])
        power = sb("power", [128, NB])
        expert_no = sb("expert_no", [128, NB, E])

        x_in = [sb(f"x_in{i}", [128, NB, D]) for i in range(2)]
        ctx_in = [sb(f"ctx_in{i}", [128, NB, KEYS]) for i in range(2)]
        stats1 = sb("stats1", [128, NB, 6])
        mv1 = [sb(f"mv1_{i}", [128, NB, 2]) for i in range(2)]
        ve1 = sb("ve1", [128, NB])
        rstd1 = [sb(f"rstd1_{i}", [128, NB]) for i in range(2)]
        xn1 = [sb(f"xn1_{i}", [128, D]) for i in range(2)]
        xT1 = sb("xT1", [128, S])
        q_rows = [sb(f"q_rows{i}", [128, HEADS, HEAD_ROWS], BF16) for i in range(2)]
        k_rows = sb("k_rows", [KEYS_E, HEADS, HEAD_ROWS], BF16)
        v_cols = [sb(f"v_cols{i}", [KEYS, HEADS, VW], BF16) for i in range(4)]
        qT = [sb(f"qT{i}", [128, HG, S], BF16) for i in range(2)]
        qmT = sb("qmT", [128, HG, S], BF16)
        kT = [sb(f"kT{i}", [128, HG, PER, KEYS], BF16) for i in range(2)]
        neg_max = sb("neg_max", [128, HEADS])
        probs = [sb(f"probs{i}", [KEYS, PER * S]) for i in range(HG)]
        probs_lo = [sb(f"probs_lo{i}", [KEYS, PER * S], BF16) for i in range(HG)]
        o_sum = sb("o_sum", [128, HEADS, DEPTH])
        o_rden = sb("o_rden", [128, HEADS])
        o_norm = sb("o_norm", [128, HEADS, DEPTH])
        x1 = [sb(f"x1_{i}", [128, NB, D]) for i in range(2)]

        stats2 = sb("stats2", [128, 6])
        mv2 = [sb(f"mv2_{i}", [128, NB, 2]) for i in range(2)]
        ve2 = sb("ve2", [128, NB])
        rstd2 = sb("rstd2", [128, NB])
        xn2 = sb("xn2", [128, NB, D])
        xT2 = [sb(f"xT2_{i}", [128, TOK]) for i in range(2)]
        xT2_rest = sb("xT2_rest", [128, TOK])
        xT2_mid = [sb(f"xT2_mid{i}", [128, TOK], BF16) for i in range(2)]
        xT2_lo = sb("xT2_lo", [128, TOK], BF16)
        logits0 = sb("logits0", [128, NB, E])
        logits = sb("logits", [128, NB, E])
        top8 = sb("top8", [128, NB, 8])
        top8_at = sb("top8_at", [128, NB, 8], U32)
        top_gap = sb("top_gap", [128, NB])
        gap_exp = sb("gap_exp", [128, NB])
        gap_one = sb("gap_one", [128, NB])
        gap_inv = sb("gap_inv", [128, NB])
        gate1 = sb("gate1", [128, NB])
        gate2 = sb("gate2", [128, NB])
        first = sb("first", [128, NB, E])
        second = sb("second", [128, NB, E])
        first_g = sb("first_g", [128, NB, E])
        second_g = sb("second_g", [128, NB, E])
        gates = [sb(f"gates{i}", [128, NB, E]) for i in range(2)]
        hidden = [sb(f"hidden{i}", [128, TOK]) for i in range(4)]
        hidden_lo = [sb(f"hidden_lo{i}", [128, TOK], BF16) for i in range(4)]
        gated = [sb(f"gated{i}", [128, NB, D]) for i in range(2)]
        acc = sb("acc", [128, NB, D])
        result = sb("result", [128, NB, D])

        def bank(name):
            return stack.enter_context(nc.psum_tensor(name, [128, 512], F32))

        score_bank = bank("scores")
        max_bank = bank("max_scores")
        hidden_bank = [bank("hidden_p0"), bank("hidden_p1")]
        y_bank = bank("y")
        o_bank = bank("o")
        bank_a = bank("bank_a")
        bank_b = bank("bank_b")

        W_LOADS = 12
        s_w = sem("weights_loaded")
        s_x = [sem("x_loaded0"), sem("x_loaded1")]
        s_ctx = [sem("ctx_loaded0"), sem("ctx_loaded1")]
        s_out = sem("out_stored")
        s_ident0, s_ident = sem("ident_cleared"), sem("ident_made")
        s_zero = sem("rows_cleared")
        s_fill = sem("constants_made")
        s_wlo = sem("weights_lo_made")
        s_b2 = sem("b2_split_step")
        s_rstd1, s_rstd2 = sem("rstd1_made"), sem("rstd2_made")
        s_mclr = sem("max_rows_cleared")
        s_hlo = sem("hidden_lo_made")
        s_acc = sem("expert_added")
        s_xlo = sem("xT2_lo_made")
        s_wr = sem("wr_split_step")
        s_st1, s_mv1, s_ve1 = sem("stats1_made"), sem("mv1_made"), sem("ve1_made")
        s_xn1 = sem("xn1_made")
        s_qlo, s_klo, s_vlo = sem("q_lo_made"), sem("k_lo_made"), sem("v_lo_made")
        s_kTd, s_kTa = sem("kT_made_by_dve"), sem("kT_made_by_act")
        s_max = sem("max_made")
        s_mhi, s_mlo = sem("max_hi_made"), sem("max_lo_made")
        s_plo = sem("probs_lo_made")
        s_osum, s_orden, s_onorm, s_x1 = sem("o_sum_made"), sem("o_rden_made"), sem("o_norm_made"), sem("x1_made")
        s_st2, s_mv2, s_ve2 = sem("stats2_made"), sem("mv2_made"), sem("ve2_made")
        s_xn2 = sem("xn2_made")
        s_xrest = sem("xT2_rest_made")
        s_logit0 = sem("logits_summed")
        s_route = sem("routing_step")
        s_gate = sem("gate_step")
        s_gates = sem("gates_made")
        s_gated = sem("expert_gated")
        s_tanh = sem("tanh_made")
        s_xT1 = sem("xT1_made")
        s_qhi, s_khi, s_vhi = sem("q_hi_made"), sem("k_hi_made"), sem("v_hi_made")
        s_qT, s_qmT = sem("qT_made"), sem("qmT_made")
        s_exp = sem("exp_made")
        s_relu = sem("hidden_made")
        s_xT2, s_xmid = sem("xT2_made"), sem("xT2_mid_made")
        s_gexp = sem("gap_exp_made")
        p_xT1, p_q, p_kv, p_qT, p_kT = (sem("pe_" + n) for n in ("xT1", "q", "kv", "qT", "kT"))
        p_max, p_qmT, p_st, p_pv = (sem("pe_" + n) for n in ("max_scores", "qmT", "scores", "values"))
        p_f1, p_f2 = sem("pe_hidden"), sem("pe_expert")
        p_xT2, p_rt = sem("pe_xT2"), sem("pe_router")

        ROUTE = 7
        FILLS = 13

        def kt_view(rows):
            return bank_b[:].bitcast(BF16)[rows, 0:HG * 80].rearrange("p (h k) -> p h k", h=HG)[:, :, 0:KEYS]

        def slots(eng, slot):
            for s in range(FIRST):
                slot(s, s, 0)
            with eng.Fori(0, (LAST - FIRST) // BODY) as it:
                for n in range(FIRST, FIRST + BODY):
                    slot(it * BODY + n, n, it)
            for s in range(LAST, SLOTS):
                slot(s, s, 0)

        def active(s, lag):
            return not isinstance(s, int) or 0 <= s - lag < B

        def group_of(n, it, lag):
            return it * (BODY // NB) + (n - lag) // NB

        def group_at(s, n, it, lag):
            if (n - lag) % NB != 0 or not active(s, lag):
                return None
            return group_of(n, it, lag)

        block = stack.enter_context(nc.Block())

        @block.sync
        def _(sp):
            x_g = x.rearrange("(g i) s d -> g s i d", i=NB)
            out_g = out.rearrange("(g i) s d -> g s i d", i=NB)
            ctx_g = ctx_t.rearrange("g d (i k) -> g d i k", i=NB)

            def load(g, par):
                if due(NB * (g - 1)):
                    sp.wait_ge(s_x1, NB * (g - 1))
                sp.dma_start(x_in[par][:], x_g[g]).then_inc(s_x[par], 16)
                if due(NB * (g - 1)):
                    sp.wait_ge(p_kv, NB * (g - 1))
                sp.dma_start(ctx_in[par][:], ctx_g[g]).then_inc(s_ctx[par], 16)

            def store(g):
                sp.wait_ge(s_acc, E * (g + 1))
                sp.dma_start(out_g[g], result[:]).then_inc(s_out, 16)

            load(0, 0)
            sp.dma_start(wq_sb[:], wq_t).then_inc(s_w, 16)
            sp.dma_start(wkv_sb[:], wkv_t).then_inc(s_w, 16)
            load(1, 1)
            sp.dma_start(gates_in[:, 0:1], g_xattn.partition_broadcast(128)).then_inc(s_w, 16)
            sp.dma_start(gates_in[:, 1:2], g_ffn.partition_broadcast(128)).then_inc(s_w, 16)
            sp.dma_start(wr_sb[:], w_router).then_inc(s_w, 16)
            sp.dma_start(br_sb[:], b_router.partition_broadcast(128)).then_inc(s_w, 16)
            sp.dma_start(b1_sb[:], b1).then_inc(s_w, 16)
            sp.dma_start(w1_sb[:], w1).then_inc(s_w, 16)
            sp.dma_start(w2_sb[:], w2).then_inc(s_w, 16)
            sp.wait_ge(s_zero, 1)
            for r in range(3):
                sp.dma_start(b2_rows[32 * r:32 * r + 1, :], b2).then_inc(s_w, 16)
            load(2, 0)
            load(3, 1)
            store(0)
            with sp.Fori(4, GROUPS - 1, 2) as g0:
                load(g0, 0)
                store(g0 - 3)
                load(g0 + 1, 1)
                store(g0 - 2)
            for g in range(GROUPS - 3, GROUPS):
                store(g)
            sp.wait_ge(s_out, 16 * GROUPS)

        @block.tensor
        def _(pe):
            mm = nc.tensor.matmul

            def x1_transpose(b, n):
                if due(b):
                    pe.wait_ge(s_qT, b)
                pe.wait_ge(s_xn1, b + 1)
                nc.tensor.transpose(bank_a[:, 0:S], xn1[n % 2][:], ident[:]).then_inc(p_xT1, 1)

            def project_q(b):
                pe.wait_ge(s_xT1, b + 1)
                mm(bank_a[:, 0:D], xT1[:], wq_sb[:], start=True, stop=True).then_inc(p_q, 1)

            def project_kv(b, n, it):
                if due(16 * (it + n // BODY + 1)):
                    pe.wait_ge(s_ctx[(n // NB) % 2], 16 * (it + n // BODY + 1))
                if due(b - 1):
                    pe.wait_ge(s_qmT, b - 1)
                if isinstance(b, int) and b >= 1:
                    if due(b):
                        pe.wait_ge(s_kTd, b)
                    if due(b):
                        pe.wait_ge(s_kTa, b)
                mm(bank_b[0:KEYS, 0:2 * D], ctx_in[(n // NB) % 2][:, n % NB, :], wkv_sb[:],
                   start=True, stop=True).then_inc(p_kv, 1)

            def transpose_q(b, n, it):
                pe.wait_ge(s_qlo, b + 1)
                if due(b - 1):
                    pe.wait_ge(s_mclr, b - 1)
                g = group_at(b, n, it, GROUP_LAG)
                if g is not None:
                    pe.wait_ge(s_xT2, g + 1)
                view = bank_a[:].bitcast(BF16)
                for h in range(HG):
                    last = nc.tensor.transpose(view[:, h * S:(h + 1) * S],
                                               q_rows[n % 2][:, h * PER:(h + 1) * PER, :], ident_b[:])
                last.then_inc(p_qT, 1)

            def transpose_k(b, n, it):
                pe.wait_ge(s_klo, b + 1)
                pe.wait_ge(s_vlo, b + 1)
                g = group_at(b, n, it, EXPERT_LAG)
                if g is not None:
                    pe.wait_ge(s_logit0, g + 1)
                view = bank_b[:].bitcast(BF16)
                for h in range(HG):
                    last = nc.tensor.transpose(view[:, h * 80:h * 80 + KEYS_E],
                                               k_rows[:, h * PER:(h + 1) * PER, :],
                                               ident_b[0:KEYS_E, 0:KEYS_E])
                last.then_inc(p_kT, 1)

            def max_scores(b, n, h):
                pe.wait_ge(s_qT, b + 1)
                pe.wait_ge(s_kTd, b + 1)
                pe.wait_ge(s_kTa, b + 1)
                if due(HG * b + h):
                    pe.wait_ge(s_max, HG * b + h)
                mm(max_bank[:, 0:PER * KEYS], qT[n % 2][:, h, :],
                   kT[n % 2][:, h, :, :], start=True, stop=True).then_inc(p_max, 1)

            def transpose_qm(b, n):
                pe.wait_ge(s_mlo, b + 1)
                made = min(b + 2, B) if isinstance(b, int) else b + 2
                pe.wait_ge(s_kTd, made)
                pe.wait_ge(s_kTa, made)
                view = bank_b[:].bitcast(BF16)
                for h in range(HG):
                    last = nc.tensor.transpose(view[:, h * S:(h + 1) * S],
                                               q_rows[n % 2][:, h * PER:(h + 1) * PER, :], ident_b[:])
                last.then_inc(p_qmT, 1)

            def scores(b, n, h):
                pe.wait_ge(s_qmT, b + 1)
                if due(HG * b + h):
                    pe.wait_ge(s_exp, HG * b + h)
                for j in range(PER):
                    last = mm(score_bank[0:KEYS, j * S:(j + 1) * S], kT[n % 2][:, h, j, :],
                              qmT[:, h, :], start=(j == 0), stop=True, skip_group_check=True)
                last.then_inc(p_st, 1)

            def values(b, n, h):
                if h == 0:
                    if due(b):
                        pe.wait_ge(s_osum, b)
                    if due(b):
                        pe.wait_ge(s_orden, b)
                pe.wait_ge(s_plo, HG * b + h + 1)
                hi = upper(probs[h][:])
                for j in range(PER):
                    head = h * PER + j
                    o = o_bank[:, head * VW:(head + 1) * VW]
                    v = v_cols[n % 4][:, head, :]
                    mm(o, hi[:, j * S:(j + 1) * S], v, start=(head == 0), stop=False,
                       skip_group_check=True)
                    last = mm(o, probs_lo[h][:, j * S:(j + 1) * S], v, start=False, stop=True,
                              skip_group_check=True)
                last.then_inc(p_pv, 1)

            def x2_transpose(g, s):
                pe.wait_ge(s_xn2, g + 1)
                if isinstance(s, int) and s >= B:
                    pass
                else:
                    pe.wait_ge(s_qlo, s + 1)
                if isinstance(s, int) and s >= B:
                    pe.wait_ge(s_qT, B)
                for i in range(NB):
                    last = nc.tensor.transpose(bank_a[:, i * S:(i + 1) * S], xn2[:, i, :], ident[:])
                last.then_inc(p_xT2, 1)

            def route(g, s, par):
                pe.wait_ge(s_xlo, g + 1)
                pe.wait_ge(s_xmid, g + 1)
                pe.wait_ge(s_wr, 6)
                if isinstance(s, int) and s >= B:
                    pe.wait_ge(s_qmT, B)
                    pe.wait_ge(s_kTd, B)
                    pe.wait_ge(s_kTa, B)
                else:
                    pe.wait_ge(s_klo, s + 1)
                    pe.wait_ge(s_vlo, s + 1)
                hi = upper(xT2[par][:])
                for i in range(NB):
                    cut = slice(i * S, (i + 1) * S)
                    o = bank_b[:, i * 3 * E:(i + 1) * 3 * E]
                    mm(o, hi[:, cut], wr3[:], start=(i == 0), stop=False, skip_group_check=True)
                    mm(o, xT2_mid[par][:, cut], wr3[:], start=False, stop=False, skip_group_check=True)
                    last = mm(o, xT2_lo[:, cut], wr3[:], start=False, stop=True, skip_group_check=True)
                last.then_inc(p_rt, 1)

            def hidden_part(t, m, par, g):
                if m == 0:
                    pe.wait_ge(s_xT2, g + 1)
                    if isinstance(g, int) and g == 0:
                        pe.wait_ge(s_wlo, 2)
                if due(t - 1):
                    pe.wait_ge(s_relu, t - 1)
                cut = slice(m * 128, (m + 1) * 128)
                o = hidden_bank[m % 2][:]
                w_hi = upper(w1_sb[:])
                mm(o, w_hi[:, cut], upper(xT2[par][:]), start=True, stop=False)
                mm(o, w1_lo[:, cut], upper(xT2[par][:]), start=False, stop=False)
                if m == 0:
                    pe.wait_ge(s_xmid, g + 1)
                mm(o, w_hi[:, cut], xT2_mid[par][:], start=False, stop=True).then_inc(p_f1, 1)

            def expert_out(e, m, tokens):
                if tokens[0] == 0:
                    if due(e):
                        pe.wait_ge(s_gated, e)
                    pe.wait_ge(s_hlo, HC * (e + 1))
                    if isinstance(e, int) and e == 0:
                        pe.wait_ge(s_b2, 5)
                    bias = b2_split[:, None, m * D:(m + 1) * D].to_broadcast([96, NB, D])
                    mm(y_bank[:], ones_b[:], bias, start=True, stop=False, skip_group_check=True)
                w_hi = upper(w2_sb[:])
                for i in tokens:
                    cut = slice(i * S, (i + 1) * S)
                    for c in range(HC):
                        k = (HC * m + c) % 4
                        w = slice((HC * m + c) * D, (HC * m + c + 1) * D)
                        hi = upper(hidden[k][:])
                        mm(y_bank[:, cut], hi[:, cut], w_hi[:, w], start=False, stop=False,
                           skip_group_check=True)
                        mm(y_bank[:, cut], hi[:, cut], w2_lo[:, w], start=False, stop=False,
                           skip_group_check=True)
                        last = mm(y_bank[:, cut], hidden_lo[k][:, cut], w_hi[:, w], start=False,
                                  stop=(c == HC - 1), skip_group_check=True)
                if tokens[-1] == NB - 1:
                    last.then_inc(p_f2, 1)

            def slot(s, n, it):
                a, b, c = active(s, 0), active(s, 1), active(s, ATT_LAG)
                f = active(s, EXPERT_LAG)
                u = s - EXPERT_LAG
                m0 = 2 * ((n - EXPERT_LAG) % NB)
                par = ((n - EXPERT_LAG) // NB) % 2
                prev = not isinstance(s, int) or 1 <= u <= B
                g2 = group_at(s, n, it, GROUP_LAG)
                gr = group_at(s, n, it, EXPERT_LAG)

                def h_part(k):
                    if f:
                        hidden_part(4 * u + k, 2 * m0 + k, par, group_of(n, it, EXPERT_LAG))

                def y_part(which, tokens):
                    if (prev if which < 0 else f):
                        expert_out(2 * u + which, (m0 + which) % E, tokens)

                if c:
                    transpose_qm(s - 2, n)
                if a:
                    x1_transpose(s, n)
                h_part(0)
                if b:
                    max_scores(s - 1, n - 1, 0)
                h_part(1)
                if c:
                    scores(s - 2, n, 0)
                if b:
                    max_scores(s - 1, n - 1, 1)
                y_part(-1, [0, 1])
                if a:
                    project_q(s)
                if c:
                    scores(s - 2, n, 1)
                if b:
                    max_scores(s - 1, n - 1, 2)
                y_part(-1, [2, 3])
                if a:
                    project_kv(s, n, it)
                if c:
                    scores(s - 2, n, 2)
                if b:
                    max_scores(s - 1, n - 1, 3)
                h_part(2)
                if c:
                    values(s - 2, n - 2, 0)
                    scores(s - 2, n, 3)
                if g2 is not None:
                    x2_transpose(g2, s)
                if gr is not None:
                    route(gr, s, par)
                h_part(3)
                if c:
                    values(s - 2, n - 2, 1)
                if a:
                    transpose_q(s, n, it)
                y_part(0, [0, 1])
                if c:
                    values(s - 2, n - 2, 2)
                if a:
                    transpose_k(s, n, it)
                y_part(0, [2, 3])
                if c:
                    values(s - 2, n - 2, 3)

            pe.wait_ge(s_w, 16 * W_LOADS)
            pe.wait_ge(s_ident, 2)
            pe.wait_ge(s_fill, FILLS)
            slots(pe, slot)

        @block.scalar
        def _(act):
            copy = nc.scalar.copy

            def exp_scores(b, n, h):
                act.wait_ge(p_st, HG * b + h + 1)
                if due(HG * (b - 1) + h + 1):
                    act.wait_ge(p_pv, HG * (b - 1) + h + 1)
                nc.scalar.activation(probs[h][:], score_bank[0:KEYS, 0:PER * S], ACT.Exp,
                                     scale=SCALE).then_inc(s_exp, 1)

            def relu(u, m0, k):
                t, e, m = 4 * u + k, 2 * u + k // HC, m0 + k
                act.wait_ge(p_f1, t + 1)
                if due(e - 1):
                    act.wait_ge(p_f2, e - 1)
                nc.scalar.activation(hidden[m % 4][:], hidden_bank[m % 2][:], ACT.Relu,
                                     bias=b1_sb[:, m:m + 1]).then_inc(s_relu, 1)

            def slot(s, n, it):
                a, c = active(s, 0), active(s, ATT_LAG)
                f = active(s, EXPERT_LAG)
                u = s - EXPERT_LAG
                m0 = 4 * ((n - EXPERT_LAG) % NB)
                g2 = group_at(s, n, it, GROUP_LAG)
                gr = group_at(s, n, it, EXPERT_LAG)
                if c:
                    if due(s - 1):
                        act.wait_ge(p_qmT, s - 1)
                    if due(HG * (s - 2)):
                        act.wait_ge(p_st, HG * (s - 2))
                    copy(qmT[:].rearrange("p h s -> p (h s)"),
                         bank_b[:].bitcast(BF16)[:, 0:HG * S]).then_inc(s_qmT, 1)
                if a:
                    act.wait_ge(p_xT1, s + 1)
                    if due(s):
                        act.wait_ge(p_q, s)
                    copy(xT1[:], bank_a[:, 0:S]).then_inc(s_xT1, 1)
                if f:
                    relu(u, m0, 0)
                if f:
                    relu(u, m0, 1)
                if c:
                    exp_scores(s - 2, n, 0)
                if a:
                    act.wait_ge(p_q, s + 1)
                    if due(s - 1):
                        act.wait_ge(p_qmT, s - 1)
                    q = bank_a[:, 0:D].rearrange("p (h d) -> p h d", h=HEADS)
                    copy(q_rows[n % 2][:, :, 0:2 * DEPTH].rearrange("p h (t d) -> p h t d", t=2),
                         q.unsqueeze(2).to_broadcast([128, HEADS, 2, DEPTH])).then_inc(s_qhi, 1)
                if c:
                    exp_scores(s - 2, n, 1)
                if a:
                    act.wait_ge(p_kv, s + 1)
                    if due(s):
                        act.wait_ge(p_kT, s)
                    k = bank_b[0:KEYS, 0:D].rearrange("p (h d) -> p h d", h=HEADS)
                    k_out = k_rows[0:KEYS, :, 0:4 * DEPTH].rearrange("p h (t d) -> p h t d", t=4)
                    copy(k_out[:, :, 0:4:2, :][:, :, 0:2, :],
                         k.unsqueeze(2).to_broadcast([KEYS, HEADS, 2, DEPTH])).then_inc(s_khi, 1)
                    if due(HG * (s - 3)):
                        act.wait_ge(p_pv, HG * (s - 3))
                    v = bank_b[0:KEYS, D:2 * D].rearrange("p (h d) -> p h d", h=HEADS)
                    copy(v_cols[n % 4][:, :, 0:DEPTH], v).then_inc(s_vhi, 1)
                if c:
                    exp_scores(s - 2, n, 2)
                if f:
                    relu(u, m0, 2)
                if c:
                    exp_scores(s - 2, n, 3)
                if g2 is not None:
                    par = ((n - GROUP_LAG) // NB) % 2
                    act.wait_ge(p_xT2, g2 + 1)
                    if due(E * HC * (g2 - 1)):
                        act.wait_ge(p_f1, E * HC * (g2 - 1))
                    copy(xT2[par][:], bank_a[:]).then_inc(s_xT2, 1)
                if f:
                    relu(u, m0, 3)
                if a:
                    act.wait_ge(p_qT, s + 1)
                    if due(HG * (s - 1)):
                        act.wait_ge(p_max, HG * (s - 1))
                    copy(qT[n % 2][:].rearrange("p h s -> p (h s)"),
                         bank_a[:].bitcast(BF16)[:, 0:HG * S]).then_inc(s_qT, 1)
                if g2 is not None:
                    act.wait_ge(s_xrest, g2 + 1)
                    copy(xT2_mid[par][:], xT2_rest[:]).then_inc(s_xmid, 1)
                if gr is not None:
                    act.wait_ge(s_route, ROUTE * gr + 3)
                    nc.scalar.activation(gap_exp[:], top_gap[:], ACT.Exp).then_inc(s_gexp, 1)
                if a:
                    act.wait_ge(p_kT, s + 1)
                    if due(HG * (s - 1)):
                        act.wait_ge(p_st, HG * (s - 1))
                    for j in range(PER // 2):
                        r = slice(HEAD_ROWS * j, HEAD_ROWS * (j + 1))
                        last = copy(kT[n % 2][r, :, j, :], kt_view(r))
                    last.then_inc(s_kTa, 1)

            act.wait_ge(s_w, 16 * W_LOADS)
            nc.scalar.activation(tanh_g[:], gates_in[:], ACT.Tanh).then_inc(s_tanh, 1)
            act.wait_ge(s_fill, FILLS)
            slots(act, slot)

        @block.vector
        def _(dve):
            V = nc.vector

            def norm1_stats(g, par, loads):
                dve.wait_ge(s_x[par], 16 * loads)
                if due(g):
                    dve.wait_ge(s_mv1, g)
                for i in range(NB):
                    last = V.bn_stats(stats1[:, i, :], x_in[par][:, i, :])
                last.then_inc(s_st1, 1)

            def norm1_mean(g, par):
                for i in range(NB):
                    last = V.bn_aggr(mv1[par][:, i, :], stats1[:, i, :])
                last.then_inc(s_mv1, 1)
                dve.wait_ge(s_mv1, g + 1)
                if due(g):
                    dve.wait_ge(s_rstd1, g)
                V.tensor_scalar_add(ve1[:], mv1[par][:, :, 1], EPS).then_inc(s_ve1, 1)

            def norm1(b, n, g):
                i, par = n % NB, (n // NB) % 2
                dve.wait_ge(s_rstd1, g + 1)
                if due(b - 1):
                    dve.wait_ge(p_xT1, b - 1)
                V.tensor_scalar(xn1[n % 2][:], x_in[par][:, i, :], mv1[par][:, i, 0:1],
                                rstd1[par][:, i:i + 1], ALU.subtract, ALU.mult).then_inc(s_xn1, 1)

            def probs_low(b, h):
                dve.wait_ge(s_exp, HG * b + h + 1)
                if due(HG * (b - 1) + h + 1):
                    dve.wait_ge(p_pv, HG * (b - 1) + h + 1)
                V.tensor_tensor(probs_lo[h][:], probs[h][:], upper(probs[h][:]),
                                ALU.subtract).then_inc(s_plo, 1)

            def head_max(b, h):
                dve.wait_ge(p_max, HG * b + h + 1)
                if h == 0:
                    if due(b):
                        dve.wait_ge(s_mlo, b)
                V.tensor_reduce(neg_max[:, h * PER:(h + 1) * PER],
                                max_bank[:, 0:PER * KEYS].rearrange("p (j k) -> p j k", j=PER),
                                AXIS_X, ALU.max, negate=True).then_inc(s_max, 1)

            def gate_expert(e, m, par, g):
                dve.wait_ge(p_f2, e + 1)
                if due(e - m % 2):
                    dve.wait_ge(s_acc, e - m % 2)
                if m == 0:
                    dve.wait_ge(s_gates, g + 1)
                V.tensor_tensor(gated[m % 2][:], y_bank[:].rearrange("p (i d) -> p i d", i=NB),
                                gates[par][:, :, m:m + 1].to_broadcast([128, NB, D]),
                                ALU.mult).then_inc(s_gated, 1)

            def route(g, par):
                r0 = ROUTE * g
                dve.wait_ge(p_rt, g + 1)
                if due(r0):
                    dve.wait_ge(s_route, r0)
                V.tensor_reduce(logits0[:], bank_b[:, 0:NB * 3 * E].rearrange(
                    "p (i t e) -> p i e t", i=NB, t=3), AXIS_X, ALU.add).then_inc(s_logit0, 1)
                dve.wait_ge(s_logit0, g + 1)
                if due(g):
                    dve.wait_ge(s_gates, g)
                V.tensor_tensor(logits[:], logits0[:], br_sb[:, None, :].to_broadcast([128, NB, E]),
                                ALU.add).then_inc(s_route, 1)

            def route_top(g):
                r0 = ROUTE * g
                for i in range(NB):
                    last = V.max(top8[:, i, :], logits[:, i, :])
                last.then_inc(s_route, 1)
                dve.wait_ge(s_route, r0 + 2)
                if due(g):
                    dve.wait_ge(s_gexp, g)
                V.tensor_tensor(top_gap[:], top8[:, :, 1], top8[:, :, 0],
                                ALU.subtract).then_inc(s_route, 1)
                for i in range(NB):
                    last = V.max_index(top8_at[:, i, :], top8[:, i, :], logits[:, i, :])
                last.then_inc(s_route, 1)
                dve.wait_ge(s_route, r0 + 4)
                V.tensor_tensor(first[:], expert_no[:], top8_at[:, :, 0:1].to_broadcast([128, NB, E]),
                                ALU.is_equal)
                V.tensor_tensor(second[:], expert_no[:], top8_at[:, :, 1:2].to_broadcast([128, NB, E]),
                                ALU.is_equal).then_inc(s_route, 1)

            def route_gates(g, par):
                r0 = ROUTE * g
                dve.wait_ge(s_gexp, g + 1)
                V.tensor_scalar_add(gap_one[:], gap_exp[:], 1.0).then_inc(s_route, 1)
                dve.wait_ge(s_route, r0 + 6)
                V.reciprocal(gap_inv[:], gap_one[:]).then_inc(s_route, 1)
                dve.wait_ge(s_route, r0 + 7)
                dve.wait_ge(s_tanh, 1)
                V.tensor_scalar(gate1[:], gap_inv[:], tanh_g[:, 1:2], None, ALU.mult).then_inc(s_gate, 1)
                dve.wait_ge(s_gate, 4 * g + 1)
                V.tensor_tensor(gate2[:], gate1[:], gap_exp[:], ALU.mult).then_inc(s_gate, 1)
                V.tensor_tensor(first_g[:], first[:], gate1[:].unsqueeze(2).to_broadcast([128, NB, E]),
                                ALU.mult).then_inc(s_gate, 1)
                dve.wait_ge(s_gate, 4 * g + 2)
                V.tensor_tensor(second_g[:], second[:], gate2[:].unsqueeze(2).to_broadcast([128, NB, E]),
                                ALU.mult).then_inc(s_gate, 1)
                dve.wait_ge(s_gate, 4 * g + 4)
                if due(E * (g - 1)):
                    dve.wait_ge(s_gated, E * (g - 1))
                V.tensor_tensor(gates[par][:], first_g[:], second_g[:], ALU.add).then_inc(s_gates, 1)

            def slot(s, n, it):
                a, b, c = active(s, 0), active(s, 1), active(s, ATT_LAG)
                u = s - EXPERT_LAG
                m0 = 2 * ((n - EXPERT_LAG) % NB)
                par = ((n - EXPERT_LAG) // NB) % 2
                loop = not isinstance(s, int)
                g2 = group_at(s, n, it, GROUP_LAG)
                gr = group_at(s, n, it, EXPERT_LAG)
                cb = s - ATT_LAG
                o = active(s, ATT_LAG + 1)
                ob, on = s - ATT_LAG - 1, n - ATT_LAG - 1
                o_par = (on // NB) % 2

                if loop or 1 <= u <= B:
                    gate_expert(2 * u - 2, (m0 - 2) % E, ((n - 1 - EXPERT_LAG) // NB) % 2,
                                group_of(n, it, EXPERT_LAG + 1))
                if o:
                    dve.wait_ge(p_pv, HG * (ob + 1))
                    if due(ob):
                        dve.wait_ge(s_onorm, ob)
                    heads = o_bank[:, 0:HEADS * VW].rearrange("p (h v) -> p h v", h=HEADS)
                    V.tensor_reduce(o_sum[:], heads[:, :, 0:2 * DEPTH].rearrange("p h (t d) -> p h d t", t=2),
                                    AXIS_X, ALU.add).then_inc(s_osum, 1)
                    V.reciprocal(o_rden[:], heads[:, :, 2 * DEPTH]).then_inc(s_orden, 1)
                if o:
                    dve.wait_ge(s_osum, ob + 1)
                    dve.wait_ge(s_orden, ob + 1)
                    if due(ob):
                        dve.wait_ge(s_x1, ob)
                    V.tensor_tensor(o_norm[:], o_sum[:], o_rden[:].unsqueeze(2).to_broadcast(
                        [128, HEADS, DEPTH]), ALU.mult).then_inc(s_onorm, 1)
                if o:
                    dve.wait_ge(s_onorm, ob + 1)
                    dve.wait_ge(s_tanh, 1)
                    if on % NB == 0:
                        if due(E * group_of(n, it, ATT_LAG + 1) - 2 * E + 1):
                            dve.wait_ge(s_acc, E * group_of(n, it, ATT_LAG + 1) - 2 * E + 1)
                    V.scalar_tensor_tensor(out=x1[o_par][:, on % NB, :],
                                           in0=o_norm[:].rearrange("p h d -> p (h d)"),
                                           scalar=tanh_g[:, 0:1], in1=x_in[o_par][:, on % NB, :],
                                           op0=ALU.mult, op1=ALU.add).then_inc(s_x1, 1)
                if o:
                    dve.wait_ge(s_x1, ob + 1)
                    if due(ob):
                        dve.wait_ge(s_mv2, ob)
                    V.bn_stats(stats2[:], x1[o_par][:, on % NB, :]).then_inc(s_st2, 1)
                if o:
                    dve.wait_ge(s_st2, ob + 1)
                if b:
                    head_max(s - 1, 0)
                if o:
                    V.bn_aggr(mv2[o_par][:, on % NB, :], stats2[:]).then_inc(s_mv2, 1)
                if g2 is not None:
                    dve.wait_ge(s_mv2, NB * (g2 + 1))
                    if due(g2):
                        dve.wait_ge(s_rstd2, g2)
                    p2 = ((n - GROUP_LAG) // NB) % 2
                    V.tensor_scalar_add(ve2[:], mv2[p2][:, :, 1], EPS).then_inc(s_ve2, 1)
                if b:
                    head_max(s - 1, 1)
                if c:
                    probs_low(cb, 0)
                if g2 is not None:
                    dve.wait_ge(s_rstd2, g2 + 1)
                    if due(g2):
                        dve.wait_ge(p_xT2, g2)
                    for i in range(NB):
                        last = V.tensor_scalar(xn2[:, i, :], x1[p2][:, i, :], mv2[p2][:, i, 0:1],
                                               rstd2[:, i:i + 1], ALU.subtract, ALU.mult)
                    last.then_inc(s_xn2, 1)
                if b:
                    head_max(s - 1, 2)
                if a:
                    dve.wait_ge(s_qhi, s + 1)
                    V.tensor_tensor(q_rows[n % 2][:, :, 2 * DEPTH:3 * DEPTH],
                                    bank_a[:, 0:D].rearrange("p (h d) -> p h d", h=HEADS),
                                    q_rows[n % 2][:, :, 0:DEPTH], ALU.subtract).then_inc(s_qlo, 1)
                if c:
                    probs_low(cb, 1)
                if loop or 1 <= u <= B:
                    gate_expert(2 * u - 1, (m0 - 1) % E, ((n - 1 - EXPERT_LAG) // NB) % 2,
                                group_of(n, it, EXPERT_LAG + 1))
                if a:
                    dve.wait_ge(s_khi, s + 1)
                    dve.wait_ge(s_vhi, s + 1)
                    V.tensor_tensor(k_rows[0:KEYS, :, DEPTH:2 * DEPTH],
                                    bank_b[0:KEYS, 0:D].rearrange("p (h d) -> p h d", h=HEADS),
                                    k_rows[0:KEYS, :, 0:DEPTH], ALU.subtract).then_inc(s_klo, 1)
                    V.tensor_tensor(v_cols[n % 4][:, :, DEPTH:2 * DEPTH],
                                    bank_b[0:KEYS, D:2 * D].rearrange("p (h d) -> p h d", h=HEADS),
                                    v_cols[n % 4][:, :, 0:DEPTH], ALU.subtract).then_inc(s_vlo, 1)
                if b:
                    head_max(s - 1, 3)
                if b:
                    bb, q = s - 1, q_rows[(n - 1) % 2]
                    dve.wait_ge(s_max, HG * (bb + 1))
                    V.tensor_copy(q[:, :, 3 * DEPTH], neg_max[:]).then_inc(s_mhi, 1)
                    dve.wait_ge(s_mhi, bb + 1)
                    V.tensor_tensor(q[:, :, 3 * DEPTH + 1], neg_max[:], q[:, :, 3 * DEPTH],
                                    ALU.subtract).then_inc(s_mlo, 1)
                if c:
                    probs_low(cb, 2)
                if (loop or 0 <= s + 1 < B):
                    norm1(s + 1, n + 1, group_of(n, it, -1))
                if gr is not None:
                    route(gr, par)
                    dve.wait_ge(s_route, ROUTE * gr + 1)
                if c:
                    probs_low(cb, 3)
                if gr is not None:
                    route_top(gr)
                if g2 is not None:
                    dve.wait_ge(s_xT2, g2 + 1)
                    if due(g2):
                        dve.wait_ge(s_xmid, g2)
                    if due(g2):
                        dve.wait_ge(s_xlo, g2)
                    V.tensor_tensor(xT2_rest[:], xT2[p2][:], upper(xT2[p2][:]),
                                    ALU.subtract).then_inc(s_xrest, 1)
                norm_next = n % NB == 2 and (loop or s < B - NB)
                if norm_next:
                    norm1_stats(group_of(n, it, 0) + 1, (n // NB + 1) % 2, it + (n // NB + 1) // 2 + 1)
                if gr is not None:
                    route_gates(gr, par)
                if norm_next:
                    dve.wait_ge(s_st1, group_of(n, it, 0) + 2)
                    if due(NB * group_of(n, it, 0)):
                        dve.wait_ge(s_xn1, NB * group_of(n, it, 0))
                if a:
                    dve.wait_ge(p_kT, s + 1)
                    if due(HG * (s - 1)):
                        dve.wait_ge(p_st, HG * (s - 1))
                    for j in range(PER // 2, PER):
                        r = slice(HEAD_ROWS * j, HEAD_ROWS * (j + 1))
                        last = V.tensor_copy(kT[n % 2][r, :, j, :], kt_view(r))
                    last.then_inc(s_kTd, 1)
                if norm_next:
                    norm1_mean(group_of(n, it, 0) + 1, (n // NB + 1) % 2)

            dve.wait_ge(s_w, 16 * W_LOADS)
            norm1_stats(0, 0, 1)
            dve.wait_ge(s_st1, 1)
            norm1_mean(0, 0)
            V.tensor_tensor(wr_rest[:], wr_sb[:], upper(wr_sb[:]), ALU.subtract).then_inc(s_wr, 1)
            V.tensor_copy(wr3[:, 0, :], upper(wr_sb[:])).then_inc(s_wr, 1)
            dve.wait_ge(s_wr, 2)
            V.tensor_tensor(wr_rest2[:], wr_rest[:], upper(wr_rest[:]), ALU.subtract).then_inc(s_wr, 1)
            V.tensor_copy(wr3[:, 1, :], upper(wr_rest[:])).then_inc(s_wr, 1)
            dve.wait_ge(s_wr, 4)
            V.tensor_copy(wr3[:, 2, :], wr_rest2[:]).then_inc(s_wr, 2)
            dve.wait_ge(s_fill, FILLS)
            norm1(0, 0, 0)
            slots(dve, slot)

        @block.gpsimd
        def _(pool):
            G = nc.gpsimd

            def hidden_low(u, m0, k):
                t, e, m = 4 * u + k, 2 * u + k // HC, 2 * m0 + k
                pool.wait_ge(s_relu, t + 1)
                if due(e - 1):
                    pool.wait_ge(p_f2, e - 1)
                G.tensor_tensor(hidden_lo[m % 4][:], hidden[m % 4][:], upper(hidden[m % 4][:]),
                                ALU.subtract).then_inc(s_hlo, 1)

            def add_expert(e, m, par, g):
                pool.wait_ge(s_gated, e + 1)
                if due(e):
                    pool.wait_ge(s_acc, e)
                if m == 0:
                    src = x1[par]
                    pool.wait_ge(s_x1, NB * (g + 1))
                else:
                    src = acc
                if m == E - 1:
                    if due(16 * g):
                        pool.wait_ge(s_out, 16 * g)
                    dst = result
                else:
                    dst = acc
                G.tensor_tensor(dst[:], gated[m % 2][:], src[:], ALU.add).then_inc(s_acc, 1)

            def slot(s, n, it):
                f = active(s, EXPERT_LAG)
                u = s - EXPERT_LAG
                m0 = 2 * ((n - EXPERT_LAG) % NB)
                loop = not isinstance(s, int)
                g2 = group_at(s, n, it, GROUP_LAG)
                prev = loop or 1 <= u <= B
                p_par = ((n - 1 - EXPERT_LAG) // NB) % 2
                p_g = group_of(n, it, EXPERT_LAG + 1)
                if g2 is not None:
                    pool.wait_ge(s_ve2, g2 + 1)
                    if due(g2):
                        pool.wait_ge(s_xn2, g2)
                    G.tensor_tensor(rstd2[:], ve2[:], power[:], ALU.pow).then_inc(s_rstd2, 1)
                if prev:
                    add_expert(2 * u - 2, (m0 - 2) % E, p_par, p_g)
                if f:
                    hidden_low(u, m0, 0)
                if active(s, ATT_LAG):
                    if due(s - 1):
                        pool.wait_ge(p_qmT, s - 1)
                if f:
                    hidden_low(u, m0, 1)
                if active(s, ATT_LAG):
                    G.memset(q_rows[n % 2][:, :, 3 * DEPTH:3 * DEPTH + 2], 0.0).then_inc(s_mclr, 1)
                if prev:
                    add_expert(2 * u - 1, (m0 - 1) % E, p_par, p_g)
                if f:
                    hidden_low(u, m0, 2)
                    hidden_low(u, m0, 3)
                if g2 is not None:
                    pool.wait_ge(s_xmid, g2 + 1)
                    if due(g2):
                        pool.wait_ge(p_rt, g2)
                    G.tensor_tensor(xT2_lo[:], xT2_rest[:], xT2_mid[((n - GROUP_LAG) // NB) % 2][:],
                                    ALU.subtract).then_inc(s_xlo, 1)
                if n % NB == 2 and (loop or s < B - NB):
                    rstd_of_norm1(group_of(n, it, 0) + 1, (n // NB + 1) % 2)

            def rstd_of_norm1(g, par):
                pool.wait_ge(s_ve1, g + 1)
                if due(NB * (g - 1)):
                    pool.wait_ge(s_xn1, NB * (g - 1))
                G.tensor_tensor(rstd1[par][:], ve1[:], power[:], ALU.pow).then_inc(s_rstd1, 1)

            G.memset(b2_rows[:], 0.0).then_inc(s_zero, 1)
            G.memset(ident[:], 0.0).then_inc(s_ident0, 1)
            G.memset(ident_b[:], 0.0).then_inc(s_ident0, 1)
            G.memset(power[:], -0.5).then_inc(s_fill, 1)
            pool.wait_ge(s_ident0, 2)
            for t in (ident, ident_b):
                G.affine_select(out=t[:], in_=t[:], compare_op=ALU.not_equal, fill=1.0, base=0,
                                pattern=[[-1, 128]], channel_multiplier=1).then_inc(s_ident, 1)
            for t in (*q_rows, *kT):
                G.memset(t[:], 0.0).then_inc(s_fill, 1)
            G.memset(k_rows[:], 0.0).then_inc(s_zero, 1)
            for t in v_cols:
                G.memset(t[:, :, 2 * DEPTH:VW], 1.0).then_inc(s_fill, 1)
            G.memset(ones_b[:], 1.0).then_inc(s_fill, 1)
            G.iota(expert_no[:], pattern=[[0, NB], [1, E]], base=0, channel_multiplier=0,
                   allow_small_or_imprecise_dtypes=True).then_inc(s_fill, 1)
            G.memset(b2_split[:], 0.0).then_inc(s_fill, 1)
            pool.wait_ge(s_zero, 2)
            G.memset(k_rows[:, :, 3 * DEPTH:3 * DEPTH + 2], 1.0).then_inc(s_fill, 1)
            pool.wait_ge(s_fill, FILLS)
            rstd_of_norm1(0, 0)
            pool.wait_ge(s_w, 16 * W_LOADS)
            G.tensor_tensor(w1_lo[:], w1_sb[:], upper(w1_sb[:]), ALU.subtract).then_inc(s_wlo, 1)
            G.tensor_tensor(w2_lo[:], w2_sb[:], upper(w2_sb[:]), ALU.subtract).then_inc(s_wlo, 1)
            G.tensor_tensor(b2_rest[:], b2_rows[:], upper(b2_rows[:]), ALU.subtract).then_inc(s_b2, 1)
            pool.wait_ge(s_b2, 1)
            G.tensor_tensor(b2_rest2[:], b2_rest[:], upper(b2_rest[:]), ALU.subtract).then_inc(s_b2, 1)
            pool.wait_ge(s_b2, 2)
            pool.wait_ge(s_b2, 2)
            G.tensor_copy(b2_split[0:1, :], upper(b2_rows[0:1, :])).then_inc(s_b2, 1)
            G.tensor_copy(b2_split[32:33, :], upper(b2_rest[32:33, :])).then_inc(s_b2, 1)
            G.tensor_copy(b2_split[64:65, :], b2_rest2[64:65, :]).then_inc(s_b2, 1)
            pool.wait_ge(s_b2, 5)
            slots(pool, slot)


def kernel(x, ctx_1024, g_xattn, g_ffn, L0_xattn_wq, L0_xattn_wk, L0_xattn_wv, L0_ffn_Wr, L0_ffn_br,
           L0_ffn_W1, L0_ffn_b1, L0_ffn_W2, L0_ffn_b2):
    import numpy as np
    import concourse.bacc as bacc
    from concourse.bass_utils import run_bass_kernel_spmd

    x = np.asarray(x)
    ctx = np.asarray(ctx_1024)
    B, K, D = ctx.shape
    E, _, H = np.asarray(L0_ffn_W1).shape
    group = 4
    arrays = {
        "x": x,
        "ctx_t": ctx.reshape(B // group, group, K, D).transpose(0, 3, 1, 2).reshape(B // group, D, group * K),
        "g_xattn": np.asarray(g_xattn), "g_ffn": np.asarray(g_ffn),
        "wq_t": np.asarray(L0_xattn_wq).T,
        "wkv_t": np.concatenate([np.asarray(L0_xattn_wk).T, np.asarray(L0_xattn_wv).T], axis=1),
        "w_router": np.asarray(L0_ffn_Wr), "b_router": np.asarray(L0_ffn_br),
        "w1": np.asarray(L0_ffn_W1).transpose(1, 0, 2).reshape(D, E * H),
        "b1": np.asarray(L0_ffn_b1).reshape(E * H // 128, 128).T,
        "w2": np.asarray(L0_ffn_W2).reshape(E * H // 128, 128, D).transpose(1, 0, 2).reshape(128, E * H // 128 * D),
        "b2": np.asarray(L0_ffn_b2).reshape(1, E * D),
    }
    arrays = {k: np.ascontiguousarray(v) for k, v in arrays.items()}
    nc = bacc.Bacc("TRN2", target_bir_lowering=False, num_devices=1)
    aps = [nc.dram_tensor(k, v.shape, mybir.dt.from_np(v.dtype), kind="ExternalInput").ap()
           for k, v in arrays.items()]
    out = nc.dram_tensor("out", x.shape, F32, kind="ExternalOutput").ap()
    flamingo_kernel(nc, *aps, out)
    r = run_bass_kernel_spmd(nc, [arrays], core_ids=[0])
    return r.results[0]["out"]
```

```python
from contextlib import ExitStack

import concourse.bass as bass
from concourse import mybir

ALU = mybir.AluOpType
ACT = mybir.ActivationFunctionType
AXIS_X = mybir.AxisListType.X
F32 = mybir.dt.float32
BF16 = mybir.dt.bfloat16
U32 = mybir.dt.uint32

EPS = 1e-5
HEAD_ROWS = 32
ATT_LAG = 2
GROUP_LAG = 6
EXPERT_LAG = 7


def upper(ap):
    return ap.bitcast(BF16).rearrange("p (n t) -> p n t", t=2)[:, :, 1]


def due(count):
    return not isinstance(count, int) or count > 0


def flamingo_kernel(nc, x, ctx_t, g_xattn, g_ffn, w_att_t, w_router, b_router, w1, b1, w2, b2, out):
    B, S, D = x.shape
    GROUPS, _, KEYS4 = ctx_t.shape
    NB = B // GROUPS
    KEYS = KEYS4 // NB
    KEYS_E = KEYS + KEYS % 2
    HEADS, DEPTH = 16, D // 16
    PER = 128 // HEAD_ROWS
    HG = HEADS // PER
    E = w_router.shape[1]
    HID = w1.shape[1] // E
    HC = HID // 128
    TOK = NB * S
    VW = 2 * DEPTH + 1
    SCALE = 1.0 / float(DEPTH) ** 0.5
    assert S == 128 and D == 128 and PER * HG == HEADS and E == 2 * NB
    SLOTS = B + EXPERT_LAG + 1
    BODY = 2 * NB
    FIRST = EXPERT_LAG + NB + 1
    LAST = B - NB
    assert (LAST - FIRST) % BODY == 0

    with ExitStack() as stack:
        def sb(name, shape, dt=F32):
            return stack.enter_context(nc.sbuf_tensor(name, shape, dt))

        def sem(name):
            return stack.enter_context(nc.semaphore(name))

        ident = sb("ident", [128, 128])
        ident_b = sb("ident_b", [128, 128], BF16)
        w_att = sb("w_att", [128, 3 * D])
        wq_sb, wkv_sb = w_att[:, 0:D], w_att[:, D:3 * D]
        w1_sb = sb("w1_sb", [128, E * HID])
        w1_lo = sb("w1_lo", [128, E * HID], BF16)
        w2_sb = sb("w2_sb", [128, E * HC * D])
        w2_lo = sb("w2_lo", [128, E * HC * D], BF16)
        wr_sb = sb("wr_sb", [128, E])
        wr_rest = sb("wr_rest", [128, E])
        wr_rest2 = sb("wr_rest2", [128, E])
        wr3 = sb("wr3", [128, 3, E], BF16)
        br_sb = sb("br_sb", [128, E])
        b1_sb = sb("b1_sb", [128, E * HC])
        b2_rows = sb("b2_rows", [96, E * D])
        b2_rest = sb("b2_rest", [96, E * D])
        b2_rest2 = sb("b2_rest2", [96, E * D])
        b2_mid = sb("b2_mid", [96, E * D], BF16)
        b2_split = sb("b2_split", [96, E * D], BF16)
        ones_b = sb("ones_b", [96, 128], BF16)
        gates_in = sb("gates_in", [128, 2])
        tanh_g = sb("tanh_g", [128, 2])
        power = sb("power", [128, 1])
        expert_no = sb("expert_no", [128, NB, E])

        x_in = [sb(f"x_in{i}", [128, NB, D]) for i in range(2)]
        ctx_in = [sb(f"ctx_in{i}", [128, NB, KEYS]) for i in range(2)]
        stats1 = sb("stats1", [128, 6])
        mv1 = [sb(f"mv1_{i}", [128, 2]) for i in range(2)]
        ve1 = sb("ve1", [128, 1])
        rstd1 = [sb(f"rstd1_{i}", [128, 1]) for i in range(2)]
        xn1 = [sb(f"xn1_{i}", [128, D]) for i in range(2)]
        xT1 = sb("xT1", [128, S])
        q_rows = [sb(f"q_rows{i}", [128, HEADS, HEAD_ROWS], BF16) for i in range(2)]
        k_rows = sb("k_rows", [KEYS_E, HEADS, HEAD_ROWS], BF16)
        v_cols = [sb(f"v_cols{i}", [KEYS, HEADS, VW], BF16) for i in range(4)]
        qT = [sb(f"qT{i}", [128, HG, S], BF16) for i in range(2)]
        qmT = sb("qmT", [128, HG, S], BF16)
        kT = [sb(f"kT{i}", [128, HG, PER, KEYS], BF16) for i in range(2)]
        neg_max = sb("neg_max", [128, HEADS])
        probs = [sb(f"probs{i}", [KEYS, PER * S]) for i in range(HG)]
        probs_lo = [sb(f"probs_lo{i}", [KEYS, PER * S], BF16) for i in range(HG)]
        o_sum = sb("o_sum", [128, HEADS, DEPTH])
        o_rden = sb("o_rden", [128, HEADS])
        o_norm = sb("o_norm", [128, HEADS, DEPTH])
        x1 = [sb(f"x1_{i}", [128, NB, D]) for i in range(2)]

        stats2 = sb("stats2", [128, 6])
        mv2 = sb("mv2", [128, 2])
        ve2 = sb("ve2", [128, 1])
        rstd2 = sb("rstd2", [128, 1])
        xn2 = sb("xn2", [128, D])
        xT2 = [sb(f"xT2_{i}", [128, TOK]) for i in range(2)]
        xT2_rest = [sb(f"xT2_rest{i}", [128, TOK]) for i in range(2)]
        xT2_mid = [sb(f"xT2_mid{i}", [128, TOK], BF16) for i in range(2)]
        xT2_lo = sb("xT2_lo", [128, TOK], BF16)
        logits0 = sb("logits0", [128, NB, E])
        logits = sb("logits", [128, NB, E])
        top8 = sb("top8", [128, NB, 8])
        top8_at = sb("top8_at", [128, NB, 8], U32)
        top_gap = sb("top_gap", [128, NB])
        gap_exp = sb("gap_exp", [128, NB])
        gap_one = sb("gap_one", [128, NB])
        gap_inv = sb("gap_inv", [128, NB])
        gate1 = sb("gate1", [128, NB])
        gate2 = sb("gate2", [128, NB])
        first = sb("first", [128, NB, E])
        second = sb("second", [128, NB, E])
        first_g = sb("first_g", [128, NB, E])
        second_g = sb("second_g", [128, NB, E])
        gates = [sb(f"gates{i}", [128, NB, E]) for i in range(2)]
        hidden = [sb(f"hidden{i}", [128, TOK]) for i in range(4)]
        hidden_lo = [sb(f"hidden_lo{i}", [128, TOK], BF16) for i in range(4)]
        acc = sb("acc", [128, NB, D])
        result = sb("result", [128, NB, D])

        def bank(name):
            return stack.enter_context(nc.psum_tensor(name, [128, 512], F32))

        score_bank = bank("scores")
        max_bank = bank("max_scores")
        hidden_bank = [bank("hidden_p0"), bank("hidden_p1")]
        y_bank = bank("y")
        o_bank = bank("o")
        bank_a = bank("bank_a")
        bank_b = bank("bank_b")

        W_LOADS = 6
        s_wa = sem("attention_weights_loaded")
        s_gin = sem("gates_loaded")
        s_w = sem("other_weights_loaded")
        s_x = [sem("x_loaded0"), sem("x_loaded1")]
        s_ctx = [sem("ctx_loaded0"), sem("ctx_loaded1")]
        s_out = sem("out_stored")
        s_ident0, s_ident = sem("ident_cleared"), sem("ident_made")
        s_power = sem("power_filled")
        s_zero = sem("k_rows_cleared")
        s_fill = sem("constants_made")
        s_wlo = sem("weights_lo_made")
        s_b2 = sem("b2_split_step")
        s_rstd1, s_rstd2 = sem("rstd1_made"), sem("rstd2_made")
        s_mclr = sem("max_rows_cleared")
        s_hlo = sem("hidden_lo_made")
        s_xlo = sem("xT2_lo_made")
        s_plo_pool = sem("probs_lo_made_by_pool")
        s_wr = sem("wr_split_step")
        s_st1, s_mv1, s_ve1 = sem("stats1_made"), sem("mv1_made"), sem("ve1_made")
        s_xn1 = sem("xn1_made")
        s_qlo, s_klo, s_vlo = sem("q_lo_made"), sem("k_lo_made"), sem("v_lo_made")
        s_kT = sem("kT_made")
        s_max = sem("max_made")
        s_mhi, s_mlo = sem("max_hi_made"), sem("max_lo_made")
        s_plo = sem("probs_lo_made")
        s_osum, s_orden, s_onorm, s_x1 = sem("o_sum_made"), sem("o_rden_made"), sem("o_norm_made"), sem("x1_made")
        s_st2, s_mv2, s_ve2 = sem("stats2_made"), sem("mv2_made"), sem("ve2_made")
        s_xn2 = sem("xn2_made")
        s_xrest = sem("xT2_rest_made")
        s_logit0 = sem("logits_summed")
        s_route = sem("routing_step")
        s_gate = sem("gate_step")
        s_gates = sem("gates_made")
        s_acc = sem("expert_added")
        s_tanh = sem("tanh_made")
        s_xT1 = sem("xT1_made")
        s_qhi, s_khi, s_vhi = sem("q_hi_made"), sem("k_hi_made"), sem("v_hi_made")
        s_qT, s_qmT = sem("qT_made"), sem("qmT_made")
        s_exp = sem("exp_made")
        s_relu = sem("hidden_made")
        s_xT2, s_xmid = sem("xT2_made"), sem("xT2_mid_made")
        s_gexp = sem("gap_exp_made")
        p_xT1, p_q, p_kv, p_qT, p_kT = (sem("pe_" + n) for n in ("xT1", "q", "kv", "qT", "kT"))
        p_max, p_qmT, p_st, p_pv = (sem("pe_" + n) for n in ("max_scores", "qmT", "scores", "values"))
        p_f1, p_f2 = sem("pe_hidden"), sem("pe_expert")
        p_xT2, p_rt = sem("pe_xT2"), sem("pe_router")

        ROUTE = 7
        router_out = slice(PER * KEYS, PER * KEYS + NB * 3 * E)
        FILLS_Q0, FILLS_KV, FILLS = 1, 7, 12

        def kt_view(rows):
            return bank_b[:].bitcast(BF16)[rows, 0:HG * 80].rearrange("p (h k) -> p h k", h=HG)[:, :, 0:KEYS]

        def slots(eng, slot):
            for s in range(FIRST):
                slot(s, s, 0)
            with eng.Fori(0, (LAST - FIRST) // BODY) as it:
                for n in range(FIRST, FIRST + BODY):
                    slot(it * BODY + n, n, it)
            for s in range(LAST, SLOTS):
                slot(s, s, 0)

        def active(s, lag):
            return not isinstance(s, int) or 0 <= s - lag < B

        def group_of(n, it, lag):
            return it * (BODY // NB) + (n - lag) // NB

        def group_at(s, n, it, lag):
            if (n - lag) % NB != 0 or not active(s, lag):
                return None
            return group_of(n, it, lag)

        block = stack.enter_context(nc.Block())

        @block.sync
        def _(sp):
            x_g = x.rearrange("(g i) s d -> g s i d", i=NB)
            out_g = out.rearrange("(g i) s d -> g s i d", i=NB)
            ctx_g = ctx_t.rearrange("g d (i k) -> g d i k", i=NB)

            def load(g, par):
                if due(NB * (g - 1)):
                    sp.wait_ge(s_x1, NB * (g - 1))
                sp.dma_start(x_in[par][:], x_g[g]).then_inc(s_x[par], 16)
                if due(NB * (g - 1)):
                    sp.wait_ge(p_kv, NB * (g - 1))
                sp.dma_start(ctx_in[par][:], ctx_g[g]).then_inc(s_ctx[par], 16)

            def store(g):
                sp.wait_ge(s_acc, E * (g + 1))
                sp.dma_start(out_g[g], result[:]).then_inc(s_out, 16)

            load(0, 0)
            sp.dma_start(w_att[:], w_att_t).then_inc(s_wa, 16)
            load(1, 1)
            sp.dma_start(w1_sb[:], w1).then_inc(s_w, 16)
            sp.dma_start(w2_sb[:], w2).then_inc(s_w, 16)
            load(2, 0)
            load(3, 1)
            store(0)
            with sp.Fori(4, GROUPS - 1, 2) as g0:
                load(g0, 0)
                store(g0 - 3)
                load(g0 + 1, 1)
                store(g0 - 2)
            for g in range(GROUPS - 3, GROUPS):
                store(g)
            sp.wait_ge(s_out, 16 * GROUPS)

        @block.tensor
        def _(pe):
            mm = nc.tensor.matmul

            def x1_transpose(b, n):
                if due(b - 1):
                    pe.wait_ge(s_qmT, b - 1)
                elif due(b):
                    pe.wait_ge(s_qT, b)
                pe.wait_ge(s_xn1, b + 1)
                nc.tensor.transpose(bank_a[:, 0:S], xn1[n % 2][:], ident[:]).then_inc(p_xT1, 1)

            def project_q(b):
                pe.wait_ge(s_xT1, b + 1)
                mm(bank_a[:, 0:D], xT1[:], wq_sb, start=True, stop=True).then_inc(p_q, 1)

            def project_kv(b, n, it):
                pe.wait_ge(s_ctx[(n // NB) % 2], 16 * (it + n // BODY + 1))
                if due(b):
                    pe.wait_ge(s_kT, b)
                mm(bank_b[0:KEYS, 0:2 * D], ctx_in[(n // NB) % 2][:, n % NB, :], wkv_sb,
                   start=True, stop=True).then_inc(p_kv, 1)

            def transpose_q(b, n):
                pe.wait_ge(s_qlo, b + 1)
                if due(b - 1):
                    pe.wait_ge(s_mclr, b - 1)
                view = bank_a[:].bitcast(BF16)
                for h in range(HG):
                    last = nc.tensor.transpose(view[:, h * S:(h + 1) * S],
                                               q_rows[n % 2][:, h * PER:(h + 1) * PER, :], ident_b[:])
                last.then_inc(p_qT, 1)

            def x2_transpose(b, kv_done):
                pe.wait_ge(s_xn2, b + 1)
                if kv_done is not None:
                    pe.wait_ge(s_klo, kv_done)
                    pe.wait_ge(s_vlo, kv_done)
                elif due(b):
                    pe.wait_ge(s_xT2, b)
                    pe.wait_ge(s_kT, B)
                nc.tensor.transpose(bank_b[:, 0:S], xn2[:], ident[:]).then_inc(p_xT2, 1)

            def transpose_k(b):
                pe.wait_ge(s_klo, b + 1)
                pe.wait_ge(s_vlo, b + 1)
                if due(b - ATT_LAG):
                    pe.wait_ge(s_xT2, b - ATT_LAG)
                view = bank_b[:].bitcast(BF16)
                for h in range(HG):
                    last = nc.tensor.transpose(view[:, h * 80:h * 80 + KEYS_E],
                                               k_rows[:, h * PER:(h + 1) * PER, :],
                                               ident_b[0:KEYS_E, 0:KEYS_E])
                last.then_inc(p_kT, 1)

            def max_scores(b, n, h):
                pe.wait_ge(s_qT, b + 1)
                pe.wait_ge(s_kT, b + 1)
                if due(HG * b + h):
                    pe.wait_ge(s_max, HG * b + h)
                mm(max_bank[:, 0:PER * KEYS], qT[n % 2][:, h, :],
                   kT[n % 2][:, h, :, :], start=True, stop=True).then_inc(p_max, 1)

            def transpose_qm(b, n):
                pe.wait_ge(s_mlo, b + 1)
                pe.wait_ge(s_qT, min(b + 2, B) if isinstance(b, int) else b + 2)
                view = bank_a[:].bitcast(BF16)
                for h in range(HG):
                    last = nc.tensor.transpose(view[:, h * S:(h + 1) * S],
                                               q_rows[n % 2][:, h * PER:(h + 1) * PER, :], ident_b[:])
                last.then_inc(p_qmT, 1)

            def scores(b, n, h):
                pe.wait_ge(s_qmT, b + 1)
                if due(HG * b + h):
                    pe.wait_ge(s_exp, HG * b + h)
                for j in range(PER):
                    last = mm(score_bank[0:KEYS, j * S:(j + 1) * S], kT[n % 2][:, h, j, :],
                              qmT[:, h, :], start=(j == 0), stop=True, skip_group_check=True)
                last.then_inc(p_st, 1)

            def values(b, n, h):
                if h == 0:
                    if due(b):
                        pe.wait_ge(s_osum, b)
                    if due(b):
                        pe.wait_ge(s_orden, b)
                pe.wait_ge((s_plo_pool, s_plo)[h % 2], HG // 2 * b + h // 2 + 1)
                hi = upper(probs[h][:])
                for j in range(PER):
                    head = h * PER + j
                    o = o_bank[:, head * VW:(head + 1) * VW]
                    v = v_cols[n % 4][:, head, :]
                    mm(o, hi[:, j * S:(j + 1) * S], v, start=(head == 0), stop=False,
                       skip_group_check=True)
                    last = mm(o, probs_lo[h][:, j * S:(j + 1) * S], v, start=False, stop=True,
                              skip_group_check=True)
                last.then_inc(p_pv, 1)

            def route(g, s, par):
                pe.wait_ge(s_xlo, NB * (g + 1))
                pe.wait_ge(s_xmid, NB * (g + 1))
                pe.wait_ge(s_wr, 6)
                if active(s, 1):
                    pe.wait_ge(s_max, HG * (s - 1) + 1)
                else:
                    pe.wait_ge(s_max, HG * B)
                if due(g):
                    pe.wait_ge(s_logit0, g)
                pe.wait_ge(s_xT2, NB * (g + 1))
                hi = upper(xT2[par][:])
                for i in range(NB):
                    cut = slice(i * S, (i + 1) * S)
                    o = max_bank[:, router_out][:, i * 3 * E:(i + 1) * 3 * E]
                    mm(o, hi[:, cut], wr3[:], start=(i == 0), stop=False, skip_group_check=True)
                    mm(o, xT2_mid[par][:, cut], wr3[:], start=False, stop=False, skip_group_check=True)
                    last = mm(o, xT2_lo[:, cut], wr3[:], start=False, stop=True, skip_group_check=True)
                last.then_inc(p_rt, 1)

            def hidden_part(t, m, par, g):
                if m == 0:
                    pe.wait_ge(s_xT2, NB * (g + 1))
                    if isinstance(g, int) and g == 0:
                        pe.wait_ge(s_wlo, 4)
                if due(t - 1):
                    pe.wait_ge(s_relu, t - 1)
                cut = slice(m * 128, (m + 1) * 128)
                o = hidden_bank[m % 2][:]
                w_hi = upper(w1_sb[:])
                mm(o, w_hi[:, cut], upper(xT2[par][:]), start=True, stop=False)
                mm(o, w1_lo[:, cut], upper(xT2[par][:]), start=False, stop=False)
                if m == 0:
                    pe.wait_ge(s_xmid, NB * (g + 1))
                mm(o, w_hi[:, cut], xT2_mid[par][:], start=False, stop=True).then_inc(p_f1, 1)

            def expert_out(e, m, tokens):
                if tokens[0] == 0:
                    if due(e):
                        pe.wait_ge(s_acc, e)
                    pe.wait_ge(s_hlo, HC * (e + 1))
                    if isinstance(e, int) and e == 0:
                        pe.wait_ge(s_b2, 5)
                        pe.wait_ge(s_fill, FILLS)
                    bias = b2_split[:, None, m * D:(m + 1) * D].to_broadcast([96, NB, D])
                    mm(y_bank[:], ones_b[:], bias, start=True, stop=False, skip_group_check=True)
                w_hi = upper(w2_sb[:])
                for i in tokens:
                    cut = slice(i * S, (i + 1) * S)
                    for c in range(HC):
                        k = (HC * m + c) % 4
                        w = slice((HC * m + c) * D, (HC * m + c + 1) * D)
                        hi = upper(hidden[k][:])
                        mm(y_bank[:, cut], hi[:, cut], w_hi[:, w], start=False, stop=False,
                           skip_group_check=True)
                        mm(y_bank[:, cut], hi[:, cut], w2_lo[:, w], start=False, stop=False,
                           skip_group_check=True)
                        last = mm(y_bank[:, cut], hidden_lo[k][:, cut], w_hi[:, w], start=False,
                                  stop=(c == HC - 1), skip_group_check=True)
                if tokens[-1] == NB - 1:
                    last.then_inc(p_f2, 1)

            def slot(s, n, it):
                a, b, c = active(s, 0), active(s, 1), active(s, ATT_LAG)
                f = active(s, EXPERT_LAG)
                u = s - EXPERT_LAG
                m0 = 2 * ((n - EXPERT_LAG) % NB)
                par = ((n - EXPERT_LAG) // NB) % 2
                prev = not isinstance(s, int) or 1 <= u <= B
                o = active(s, ATT_LAG + 1)
                gr = group_at(s, n, it, EXPERT_LAG)

                def h_part(k):
                    if f:
                        hidden_part(4 * u + k, 2 * m0 + k, par, group_of(n, it, EXPERT_LAG))

                def y_part(which, tokens):
                    if (prev if which < 0 else f):
                        expert_out(2 * u + which, (m0 + which) % E, tokens)

                h_part(0)
                if a:
                    x1_transpose(s, n)
                if b:
                    max_scores(s - 1, n - 1, 0)
                h_part(1)
                if c:
                    scores(s - 2, n, 0)
                if gr is not None:
                    route(gr, s, par)
                if b:
                    max_scores(s - 1, n - 1, 1)
                y_part(-1, [0, 1])
                if a:
                    project_q(s)
                if c:
                    scores(s - 2, n, 1)
                if b:
                    max_scores(s - 1, n - 1, 2)
                y_part(-1, [2, 3])
                if a:
                    project_kv(s, n, it)
                if c:
                    scores(s - 2, n, 2)
                if b:
                    max_scores(s - 1, n - 1, 3)
                h_part(2)
                if c:
                    values(s - 2, n - 2, 0)
                    scores(s - 2, n, 3)
                h_part(3)
                if c:
                    values(s - 2, n - 2, 1)
                if a:
                    transpose_q(s, n)
                if o:
                    x2_transpose(s - 3, s + 1 if a else None)
                y_part(0, [0, 1])
                if b:
                    transpose_qm(s - 1, n - 1)
                if a:
                    transpose_k(s)
                if c:
                    values(s - 2, n - 2, 2)
                y_part(0, [2, 3])
                if c:
                    values(s - 2, n - 2, 3)

            pe.wait_ge(s_wa, 16)
            pe.wait_ge(s_ident, 2)
            slots(pe, slot)

        @block.scalar
        def _(act):
            copy = nc.scalar.copy

            def exp_scores(b, n, h):
                act.wait_ge(p_st, HG * b + h + 1)
                if due(HG * (b - 1) + h + 1):
                    act.wait_ge(p_pv, HG * (b - 1) + h + 1)
                nc.scalar.activation(probs[h][:], score_bank[0:KEYS, 0:PER * S], ACT.Exp,
                                     scale=SCALE).then_inc(s_exp, 1)

            def relu(u, m0, k):
                t, e, m = 4 * u + k, 2 * u + k // HC, m0 + k
                act.wait_ge(p_f1, t + 1)
                if due(e - 1):
                    act.wait_ge(p_f2, e - 1)
                nc.scalar.activation(hidden[m % 4][:], hidden_bank[m % 2][:], ACT.Relu,
                                     bias=b1_sb[:, m:m + 1]).then_inc(s_relu, 1)

            def slot(s, n, it):
                a, c = active(s, 0), active(s, ATT_LAG)
                f = active(s, EXPERT_LAG)
                u = s - EXPERT_LAG
                m0 = 4 * ((n - EXPERT_LAG) % NB)
                o = active(s, ATT_LAG + 1)
                x_par, x_i = ((n - 3) // NB) % 2, (n - 3) % NB
                gr = group_at(s, n, it, EXPERT_LAG)
                if n == 4:
                    act.wait_ge(s_b2, 2)
                    act.wait_ge(s_fill, FILLS)
                    copy(b2_split[0:1, :], upper(b2_rows[0:1, :])).then_inc(s_b2, 1)
                    copy(b2_split[32:33, :], upper(b2_rest[32:33, :])).then_inc(s_b2, 1)
                    copy(b2_split[64:65, :], b2_rest2[64:65, :]).then_inc(s_b2, 1)
                if a:
                    act.wait_ge(p_xT1, s + 1)
                    if due(s):
                        act.wait_ge(p_q, s)
                    copy(xT1[:], bank_a[:, 0:S]).then_inc(s_xT1, 1)
                if f:
                    relu(u, m0, 0)
                if f:
                    relu(u, m0, 1)
                if c:
                    exp_scores(s - 2, n, 0)
                if a:
                    act.wait_ge(p_q, s + 1)
                    if due(s - 1):
                        act.wait_ge(p_qmT, s - 1)
                    if n == 0:
                        act.wait_ge(s_fill, FILLS_Q0)
                    if n == 1:
                        act.wait_ge(s_fill, FILLS)
                    q = bank_a[:, 0:D].rearrange("p (h d) -> p h d", h=HEADS)
                    copy(q_rows[n % 2][:, :, 0:2 * DEPTH].rearrange("p h (t d) -> p h t d", t=2),
                         q.unsqueeze(2).to_broadcast([128, HEADS, 2, DEPTH])).then_inc(s_qhi, 1)
                if c:
                    exp_scores(s - 2, n, 1)
                if a:
                    act.wait_ge(p_kv, s + 1)
                    if due(s):
                        act.wait_ge(p_kT, s)
                    if n == 0:
                        act.wait_ge(s_fill, FILLS_KV)
                    k = bank_b[0:KEYS, 0:D].rearrange("p (h d) -> p h d", h=HEADS)
                    k_out = k_rows[0:KEYS, :, 0:4 * DEPTH].rearrange("p h (t d) -> p h t d", t=4)
                    copy(k_out[:, :, 0:4:2, :][:, :, 0:2, :],
                         k.unsqueeze(2).to_broadcast([KEYS, HEADS, 2, DEPTH])).then_inc(s_khi, 1)
                    if due(HG * (s - 3)):
                        act.wait_ge(p_pv, HG * (s - 3))
                    v = bank_b[0:KEYS, D:2 * D].rearrange("p (h d) -> p h d", h=HEADS)
                    copy(v_cols[n % 4][:, :, 0:DEPTH], v).then_inc(s_vhi, 1)
                if gr is not None:
                    act.wait_ge(s_route, ROUTE * gr + 3)
                    nc.scalar.activation(gap_exp[:], top_gap[:], ACT.Exp).then_inc(s_gexp, 1)
                if c:
                    exp_scores(s - 2, n, 2)
                if f:
                    relu(u, m0, 2)
                if c:
                    exp_scores(s - 2, n, 3)
                if f:
                    relu(u, m0, 3)
                if a:
                    act.wait_ge(p_qT, s + 1)
                    if due(HG * (s - 1)):
                        act.wait_ge(p_max, HG * (s - 1))
                    copy(qT[n % 2][:].rearrange("p h s -> p (h s)"),
                         bank_a[:].bitcast(BF16)[:, 0:HG * S]).then_inc(s_qT, 1)
                if o:
                    act.wait_ge(p_xT2, s - 2)
                    copy(xT2[x_par][:, x_i * S:(x_i + 1) * S], bank_b[:, 0:S]).then_inc(s_xT2, 1)
                if active(s, 1):
                    act.wait_ge(p_qmT, s)
                    if due(HG * (s - 1)):
                        act.wait_ge(p_st, HG * (s - 1))
                    copy(qmT[:].rearrange("p h s -> p (h s)"),
                         bank_a[:].bitcast(BF16)[:, 0:HG * S]).then_inc(s_qmT, 1)
                if a:
                    act.wait_ge(p_kT, s + 1)
                    if due(HG * (s - 1)):
                        act.wait_ge(p_st, HG * (s - 1))
                    for j in range(PER):
                        r = slice(HEAD_ROWS * j, HEAD_ROWS * (j + 1))
                        last = copy(kT[n % 2][r, :, j, :], kt_view(r))
                    last.then_inc(s_kT, 1)
                if o:
                    act.wait_ge(s_xrest, s - 2)
                    copy(xT2_mid[x_par][:, x_i * S:(x_i + 1) * S],
                         xT2_rest[x_par][:, x_i * S:(x_i + 1) * S]).then_inc(s_xmid, 1)

            act.dma_start(gates_in[:, 0:1], g_xattn.partition_broadcast(128)).then_inc(s_gin, 16)
            act.dma_start(gates_in[:, 1:2], g_ffn.partition_broadcast(128)).then_inc(s_gin, 16)
            act.dma_start(wr_sb[:], w_router).then_inc(s_w, 16)
            act.dma_start(br_sb[:], b_router.partition_broadcast(128)).then_inc(s_w, 16)
            act.dma_start(b1_sb[:], b1).then_inc(s_w, 16)
            act.dma_start(b2_rows[:], b2.partition_broadcast(96)).then_inc(s_w, 16)
            act.wait_ge(s_gin, 32)
            nc.scalar.activation(tanh_g[:], gates_in[:], ACT.Tanh).then_inc(s_tanh, 1)
            slots(act, slot)

        @block.vector
        def _(dve):
            V = nc.vector

            def norm1_stats(b, n, loads):
                dve.wait_ge(s_x[(n // NB) % 2], 16 * loads)
                if due(b):
                    dve.wait_ge(s_mv1, b)
                V.bn_stats(stats1[:], x_in[(n // NB) % 2][:, n % NB, :]).then_inc(s_st1, 1)

            def norm1_mean(n):
                V.bn_aggr(mv1[n % 2][:], stats1[:]).then_inc(s_mv1, 1)

            def norm1_var(b, n):
                dve.wait_ge(s_mv1, b + 1)
                if due(b):
                    dve.wait_ge(s_rstd1, b)
                V.tensor_scalar_add(ve1[:], mv1[n % 2][:, 1:2], EPS).then_inc(s_ve1, 1)

            def norm1(b, n):
                dve.wait_ge(s_rstd1, b + 1)
                if due(b - 1):
                    dve.wait_ge(p_xT1, b - 1)
                V.tensor_scalar(xn1[n % 2][:], x_in[(n // NB) % 2][:, n % NB, :], mv1[n % 2][:, 0:1],
                                rstd1[n % 2][:], ALU.subtract, ALU.mult).then_inc(s_xn1, 1)

            def probs_low(b, h):
                dve.wait_ge(s_exp, HG * b + h + 1)
                if due(HG * (b - 1) + h + 1):
                    dve.wait_ge(p_pv, HG * (b - 1) + h + 1)
                V.tensor_tensor(probs_lo[h][:], probs[h][:], upper(probs[h][:]),
                                ALU.subtract).then_inc(s_plo, 1)

            def head_max(b, h):
                dve.wait_ge(p_max, HG * b + h + 1)
                if h == 0:
                    if due(b):
                        dve.wait_ge(s_mlo, b)
                V.tensor_reduce(neg_max[:, h * PER:(h + 1) * PER],
                                max_bank[:, 0:PER * KEYS].rearrange("p (j k) -> p j k", j=PER),
                                AXIS_X, ALU.max, negate=True).then_inc(s_max, 1)

            def add_expert(e, m, par, g):
                dve.wait_ge(p_f2, e + 1)
                src, dst = (x1[par] if m == 0 else acc), (result if m == E - 1 else acc)
                if m == 0:
                    dve.wait_ge(s_gates, g + 1)
                else:
                    dve.wait_ge(s_acc, e)
                if m == E - 1:
                    if due(16 * g):
                        dve.wait_ge(s_out, 16 * g)
                for i in range(NB):
                    last = V.scalar_tensor_tensor(
                        out=dst[:, i, :], in0=y_bank[:, i * D:(i + 1) * D], scalar=gates[par][:, i, m:m + 1],
                        in1=src[:, i, :], op0=ALU.mult, op1=ALU.add)
                last.then_inc(s_acc, 1)

            def logits_sum(g, s):
                r0 = ROUTE * g
                dve.wait_ge(p_rt, g + 1)
                if active(s, 1):
                    dve.wait_ge(p_max, HG * (s - 1) + 2)
                if due(r0):
                    dve.wait_ge(s_route, r0)
                V.tensor_reduce(logits0[:], max_bank[:, router_out].rearrange(
                    "p (i t e) -> p i e t", i=NB, t=3), AXIS_X, ALU.add).then_inc(s_logit0, 1)

            def logits_bias(g):
                dve.wait_ge(s_logit0, g + 1)
                if due(g):
                    dve.wait_ge(s_gates, g)
                V.tensor_tensor(logits[:], logits0[:], br_sb[:, None, :].to_broadcast([128, NB, E]),
                                ALU.add).then_inc(s_route, 1)

            def route_max(g):
                for i in range(NB):
                    last = V.max(top8[:, i, :], logits[:, i, :])
                last.then_inc(s_route, 1)

            def route_gap(g):
                dve.wait_ge(s_route, ROUTE * g + 2)
                if due(g):
                    dve.wait_ge(s_gexp, g)
                V.tensor_tensor(top_gap[:], top8[:, :, 1], top8[:, :, 0],
                                ALU.subtract).then_inc(s_route, 1)

            def route_index(g):
                for i in range(NB):
                    last = V.max_index(top8_at[:, i, :], top8[:, i, :], logits[:, i, :])
                last.then_inc(s_route, 1)

            def route_masks(g):
                dve.wait_ge(s_route, ROUTE * g + 4)
                V.tensor_tensor(first[:], expert_no[:], top8_at[:, :, 0:1].to_broadcast([128, NB, E]),
                                ALU.is_equal)
                V.tensor_tensor(second[:], expert_no[:], top8_at[:, :, 1:2].to_broadcast([128, NB, E]),
                                ALU.is_equal).then_inc(s_route, 1)

            def gate_sum(g):
                dve.wait_ge(s_gexp, g + 1)
                V.tensor_scalar_add(gap_one[:], gap_exp[:], 1.0).then_inc(s_route, 1)

            def gate_inverse(g):
                dve.wait_ge(s_route, ROUTE * g + 6)
                V.reciprocal(gap_inv[:], gap_one[:]).then_inc(s_route, 1)

            def gate_first(g):
                dve.wait_ge(s_route, ROUTE * g + 7)
                dve.wait_ge(s_tanh, 1)
                V.tensor_scalar(gate1[:], gap_inv[:], tanh_g[:, 1:2], None, ALU.mult).then_inc(s_gate, 1)

            def gate_second(g):
                dve.wait_ge(s_gate, 4 * g + 1)
                V.tensor_tensor(gate2[:], gate1[:], gap_exp[:], ALU.mult).then_inc(s_gate, 1)
                V.tensor_tensor(first_g[:], first[:], gate1[:].unsqueeze(2).to_broadcast([128, NB, E]),
                                ALU.mult).then_inc(s_gate, 1)

            def gate_place_second(g):
                dve.wait_ge(s_gate, 4 * g + 2)
                V.tensor_tensor(second_g[:], second[:], gate2[:].unsqueeze(2).to_broadcast([128, NB, E]),
                                ALU.mult).then_inc(s_gate, 1)

            def gate_all(g, par):
                dve.wait_ge(s_gate, 4 * g + 4)
                if due(g - 1):
                    dve.wait_ge(s_acc, E * (g - 1))
                V.tensor_tensor(gates[par][:], first_g[:], second_g[:], ALU.add).then_inc(s_gates, 1)

            def split_experts(part):
                w, lo = ((w1_sb, w1_lo), (w2_sb, w2_lo))[part // 2]
                half = slice(part % 2 * (E * HID // 2), (part % 2 + 1) * (E * HID // 2))
                if part == 0:
                    dve.wait_ge(s_w, 16 * W_LOADS)
                V.tensor_tensor(lo[:, half], w[:, half], upper(w[:])[:, half], ALU.subtract).then_inc(s_wlo, 1)

            def split_router():
                dve.wait_ge(s_w, 16 * W_LOADS)
                V.tensor_tensor(wr_rest[:], wr_sb[:], upper(wr_sb[:]), ALU.subtract).then_inc(s_wr, 1)
                V.tensor_copy(wr3[:, 0, :], upper(wr_sb[:])).then_inc(s_wr, 1)
                dve.wait_ge(s_wr, 2)
                V.tensor_tensor(wr_rest2[:], wr_rest[:], upper(wr_rest[:]), ALU.subtract).then_inc(s_wr, 1)
                V.tensor_copy(wr3[:, 1, :], upper(wr_rest[:])).then_inc(s_wr, 1)
                dve.wait_ge(s_wr, 4)
                V.tensor_copy(wr3[:, 2, :], wr_rest2[:]).then_inc(s_wr, 2)

            def slot(s, n, it):
                a, b, c = active(s, 0), active(s, 1), active(s, ATT_LAG)
                u = s - EXPERT_LAG
                m0 = 2 * ((n - EXPERT_LAG) % NB)
                par = ((n - EXPERT_LAG) // NB) % 2
                loop = not isinstance(s, int)
                gr = group_at(s, n, it, EXPERT_LAG)
                cb = s - ATT_LAG
                o = active(s, ATT_LAG + 1)
                ob, on = s - ATT_LAG - 1, n - ATT_LAG - 1
                o_par = (on // NB) % 2

                if 3 <= n < 7:
                    split_experts(n - 3)
                if n == 4:
                    split_router()
                if n == 5:
                    dve.wait_ge(s_fill, FILLS)
                if loop or 1 <= u <= B:
                    add_expert(2 * u - 2, (m0 - 2) % E, ((n - 1 - EXPERT_LAG) // NB) % 2,
                               group_of(n, it, EXPERT_LAG + 1))
                if b:
                    head_max(s - 1, 0)
                if o:
                    dve.wait_ge(p_pv, HG * (ob + 1))
                    if due(ob):
                        dve.wait_ge(s_onorm, ob)
                    heads = o_bank[:, 0:HEADS * VW].rearrange("p (h v) -> p h v", h=HEADS)
                    V.tensor_reduce(o_sum[:], heads[:, :, 0:2 * DEPTH].rearrange("p h (t d) -> p h d t", t=2),
                                    AXIS_X, ALU.add).then_inc(s_osum, 1)
                    V.reciprocal(o_rden[:], heads[:, :, 2 * DEPTH]).then_inc(s_orden, 1)
                if gr is not None:
                    logits_sum(gr, s)
                if b:
                    head_max(s - 1, 1)
                if o:
                    dve.wait_ge(s_osum, ob + 1)
                    dve.wait_ge(s_orden, ob + 1)
                    if due(ob):
                        dve.wait_ge(s_x1, ob)
                    V.tensor_tensor(o_norm[:], o_sum[:], o_rden[:].unsqueeze(2).to_broadcast(
                        [128, HEADS, DEPTH]), ALU.mult).then_inc(s_onorm, 1)
                if loop or s + 1 < B:
                    norm1(s + 1, n + 1)
                if o:
                    dve.wait_ge(s_onorm, ob + 1)
                    dve.wait_ge(s_tanh, 1)
                    if on % NB == 0:
                        if due(E * group_of(n, it, ATT_LAG + 1) - 2 * E + 1):
                            dve.wait_ge(s_acc, E * group_of(n, it, ATT_LAG + 1) - 2 * E + 1)
                    V.scalar_tensor_tensor(out=x1[o_par][:, on % NB, :],
                                           in0=o_norm[:].rearrange("p h d -> p (h d)"),
                                           scalar=tanh_g[:, 0:1], in1=x_in[o_par][:, on % NB, :],
                                           op0=ALU.mult, op1=ALU.add).then_inc(s_x1, 1)
                if gr is not None:
                    logits_bias(gr)
                    dve.wait_ge(s_route, ROUTE * gr + 1)
                if o:
                    dve.wait_ge(s_x1, ob + 1)
                    if due(ob):
                        dve.wait_ge(s_mv2, ob)
                    V.bn_stats(stats2[:], x1[o_par][:, on % NB, :]).then_inc(s_st2, 1)
                ahead = loop or s + 2 < B
                if o:
                    dve.wait_ge(s_st2, ob + 1)
                    if due(ob):
                        dve.wait_ge(s_xn2, ob)
                if b:
                    head_max(s - 1, 2)
                if gr is not None:
                    route_max(gr)
                if o:
                    V.bn_aggr(mv2[:], stats2[:]).then_inc(s_mv2, 1)
                if gr is not None:
                    route_gap(gr)
                if gr is not None:
                    route_index(gr)
                if a:
                    dve.wait_ge(s_qhi, s + 1)
                    V.tensor_tensor(q_rows[n % 2][:, :, 2 * DEPTH:3 * DEPTH],
                                    bank_a[:, 0:D].rearrange("p (h d) -> p h d", h=HEADS),
                                    q_rows[n % 2][:, :, 0:DEPTH], ALU.subtract).then_inc(s_qlo, 1)
                if o:
                    dve.wait_ge(s_mv2, ob + 1)
                    if due(ob):
                        dve.wait_ge(s_rstd2, ob)
                    V.tensor_scalar_add(ve2[:], mv2[:, 1:2], EPS).then_inc(s_ve2, 1)
                if gr is not None:
                    route_masks(gr)
                if c:
                    probs_low(cb, 1)
                if loop or 1 <= u <= B:
                    add_expert(2 * u - 1, (m0 - 1) % E, ((n - 1 - EXPERT_LAG) // NB) % 2,
                               group_of(n, it, EXPERT_LAG + 1))
                if gr is not None:
                    gate_sum(gr)
                if o:
                    dve.wait_ge(s_rstd2, ob + 1)
                    if due(ob):
                        dve.wait_ge(p_xT2, ob)
                    V.tensor_scalar(xn2[:], x1[o_par][:, on % NB, :], mv2[:, 0:1], rstd2[:],
                                    ALU.subtract, ALU.mult).then_inc(s_xn2, 1)
                if gr is not None:
                    gate_inverse(gr)
                if a:
                    dve.wait_ge(s_khi, s + 1)
                    dve.wait_ge(s_vhi, s + 1)
                    V.tensor_tensor(k_rows[0:KEYS, :, DEPTH:2 * DEPTH],
                                    bank_b[0:KEYS, 0:D].rearrange("p (h d) -> p h d", h=HEADS),
                                    k_rows[0:KEYS, :, 0:DEPTH], ALU.subtract).then_inc(s_klo, 1)
                if gr is not None:
                    gate_first(gr)
                if a:
                    V.tensor_tensor(v_cols[n % 4][:, :, DEPTH:2 * DEPTH],
                                    bank_b[0:KEYS, D:2 * D].rearrange("p (h d) -> p h d", h=HEADS),
                                    v_cols[n % 4][:, :, 0:DEPTH], ALU.subtract).then_inc(s_vlo, 1)
                if gr is not None:
                    gate_second(gr)
                bb, q = s - 1, q_rows[(n - 1) % 2]
                if b:
                    head_max(s - 1, 3)
                if gr is not None:
                    gate_place_second(gr)
                ahead = loop or s + 2 < B
                if ahead:
                    norm1_stats(s + 2, n + 2, it + (n + 2) // BODY + 1)
                    dve.wait_ge(s_st1, s + 3)
                    if due(s + 1):
                        dve.wait_ge(s_xn1, s + 1)
                if b:
                    dve.wait_ge(s_max, HG * (bb + 1))
                    V.tensor_copy(q[:, :, 3 * DEPTH], neg_max[:]).then_inc(s_mhi, 1)
                if ahead:
                    norm1_mean(n + 2)
                if gr is not None:
                    gate_all(gr, par)
                if b:
                    dve.wait_ge(s_mhi, bb + 1)
                    V.tensor_tensor(q[:, :, 3 * DEPTH + 1], neg_max[:], q[:, :, 3 * DEPTH],
                                    ALU.subtract).then_inc(s_mlo, 1)
                if c:
                    probs_low(cb, 3)
                if ahead:
                    norm1_var(s + 2, n + 2)
                if o:
                    cols = slice((on % NB) * S, (on % NB + 1) * S)
                    dve.wait_ge(s_xT2, ob + 1)
                    V.tensor_tensor(xT2_rest[o_par][:, cols], xT2[o_par][:, cols],
                                    upper(xT2[o_par][:])[:, cols], ALU.subtract).then_inc(s_xrest, 1)

            for b in range(2):
                norm1_stats(b, b, 1)
                dve.wait_ge(s_st1, b + 1)
                norm1_mean(b)
                norm1_var(b, b)
            norm1(0, 0)
            slots(dve, slot)

        @block.gpsimd
        def _(pool):
            G = nc.gpsimd

            def hidden_low(u, m0, k):
                t, e, m = 4 * u + k, 2 * u + k // HC, 2 * m0 + k
                pool.wait_ge(s_relu, t + 1)
                if due(e - 1):
                    pool.wait_ge(p_f2, e - 1)
                G.tensor_tensor(hidden_lo[m % 4][:], hidden[m % 4][:], upper(hidden[m % 4][:]),
                                ALU.subtract).then_inc(s_hlo, 1)

            def probs_low(b, h):
                pool.wait_ge(s_exp, HG * b + h + 1)
                if due(HG * (b - 1) + h + 1):
                    pool.wait_ge(p_pv, HG * (b - 1) + h + 1)
                G.tensor_tensor(probs_lo[h][:], probs[h][:], upper(probs[h][:]),
                                ALU.subtract).then_inc(s_plo_pool, 1)

            def slot(s, n, it):
                c, f = active(s, ATT_LAG), active(s, EXPERT_LAG)
                u = s - EXPERT_LAG
                m0 = 2 * ((n - EXPERT_LAG) % NB)
                x_par, x_i = ((n - 4) // NB) % 2, (n - 4) % NB
                if n == 2:
                    split_b2()
                if n == 3:
                    split_b2_again()
                if active(s + 1, 0):
                    rstd_of_norm1(s + 1, n + 1)
                if active(s, ATT_LAG + 2):
                    pool.wait_ge(s_xmid, s - 3)
                    if x_i == 0:
                        if due(group_of(n, it, ATT_LAG + 2)):
                            pool.wait_ge(p_rt, group_of(n, it, ATT_LAG + 2))
                    cut = slice(x_i * S, (x_i + 1) * S)
                    G.tensor_tensor(xT2_lo[:, cut], xT2_rest[x_par][:, cut], xT2_mid[x_par][:, cut],
                                    ALU.subtract).then_inc(s_xlo, 1)
                if f:
                    hidden_low(u, m0, 0)
                if c:
                    if due(s - 1):
                        pool.wait_ge(p_qmT, s - 1)
                if f:
                    hidden_low(u, m0, 1)
                if c:
                    G.memset(q_rows[n % 2][:, :, 3 * DEPTH:3 * DEPTH + 2], 0.0).then_inc(s_mclr, 1)
                    probs_low(s - 2, 0)
                if active(s, ATT_LAG + 1):
                    pool.wait_ge(s_ve2, s - 2)
                    if due(s - 3):
                        pool.wait_ge(s_xn2, s - 3)
                    G.tensor_tensor(rstd2[:], ve2[:], power[:], ALU.pow).then_inc(s_rstd2, 1)
                if c:
                    probs_low(s - 2, 2)
                if f:
                    hidden_low(u, m0, 2)
                    hidden_low(u, m0, 3)

            def split_b2():
                pool.wait_ge(s_w, 16 * W_LOADS)
                G.tensor_tensor(b2_rest[:], b2_rows[:], upper(b2_rows[:]), ALU.subtract).then_inc(s_b2, 1)

            def split_b2_again():
                pool.wait_ge(s_b2, 1)
                G.tensor_tensor(b2_rest2[:], b2_rest[:], upper(b2_rest[:]), ALU.subtract).then_inc(s_b2, 1)

            def rstd_of_norm1(b, n):
                pool.wait_ge(s_ve1, b + 1)
                if due(b - 1):
                    pool.wait_ge(s_xn1, b - 1)
                G.tensor_tensor(rstd1[n % 2][:], ve1[:], power[:], ALU.pow).then_inc(s_rstd1, 1)

            G.memset(power[:], -0.5).then_inc(s_power, 1)
            G.memset(ident[:], 0.0).then_inc(s_ident0, 1)
            G.memset(ident_b[:], 0.0).then_inc(s_ident0, 1)
            pool.wait_ge(s_ident0, 2)
            for t in (ident, ident_b):
                G.affine_select(out=t[:], in_=t[:], compare_op=ALU.not_equal, fill=1.0, base=0,
                                pattern=[[-1, 128]], channel_multiplier=1).then_inc(s_ident, 1)
            pool.wait_ge(s_power, 1)
            rstd_of_norm1(0, 0)
            G.memset(q_rows[0][:], 0.0).then_inc(s_fill, 1)
            G.memset(k_rows[:], 0.0).then_inc(s_zero, 1)
            pool.wait_ge(s_zero, 1)
            G.memset(k_rows[:, :, 3 * DEPTH:3 * DEPTH + 2], 1.0).then_inc(s_fill, 1)
            for t in v_cols:
                G.memset(t[:, :, 2 * DEPTH:VW], 1.0).then_inc(s_fill, 1)
            for t in (kT[0], q_rows[1], kT[1]):
                G.memset(t[:], 0.0).then_inc(s_fill, 1)
            G.memset(ones_b[:], 1.0).then_inc(s_fill, 1)
            G.iota(expert_no[:], pattern=[[0, NB], [1, E]], base=0, channel_multiplier=0,
                   allow_small_or_imprecise_dtypes=True).then_inc(s_fill, 1)
            G.memset(b2_split[:], 0.0).then_inc(s_fill, 1)
            slots(pool, slot)


def kernel(x, ctx_1024, g_xattn, g_ffn, L0_xattn_wq, L0_xattn_wk, L0_xattn_wv, L0_ffn_Wr, L0_ffn_br,
           L0_ffn_W1, L0_ffn_b1, L0_ffn_W2, L0_ffn_b2):
    import numpy as np
    import concourse.bacc as bacc
    from concourse.bass_utils import run_bass_kernel_spmd

    x = np.asarray(x)
    ctx = np.asarray(ctx_1024)
    B, K, D = ctx.shape
    E, _, H = np.asarray(L0_ffn_W1).shape
    group = 4
    arrays = {
        "x": x,
        "ctx_t": ctx.reshape(B // group, group, K, D).transpose(0, 3, 1, 2).reshape(B // group, D, group * K),
        "g_xattn": np.asarray(g_xattn), "g_ffn": np.asarray(g_ffn),
        "w_att_t": np.concatenate([np.asarray(w).T for w in (L0_xattn_wq, L0_xattn_wk, L0_xattn_wv)], axis=1),
        "w_router": np.asarray(L0_ffn_Wr), "b_router": np.asarray(L0_ffn_br),
        "w1": np.asarray(L0_ffn_W1).transpose(1, 0, 2).reshape(D, E * H),
        "b1": np.asarray(L0_ffn_b1).reshape(E * H // 128, 128).T,
        "w2": np.asarray(L0_ffn_W2).reshape(E * H // 128, 128, D).transpose(1, 0, 2).reshape(128, E * H // 128 * D),
        "b2": np.asarray(L0_ffn_b2).reshape(E * D),
    }
    arrays = {k: np.ascontiguousarray(v) for k, v in arrays.items()}
    nc = bacc.Bacc("TRN2", target_bir_lowering=False, num_devices=1)
    aps = [nc.dram_tensor(k, v.shape, mybir.dt.from_np(v.dtype), kind="ExternalInput").ap()
           for k, v in arrays.items()]
    out = nc.dram_tensor("out", x.shape, F32, kind="ExternalOutput").ap()
    flamingo_kernel(nc, *aps, out)
    r = run_bass_kernel_spmd(nc, [arrays], core_ids=[0])
    return r.results[0]["out"]
```
